# Optimizing a Trainium2 kernel written in Bass

```python
import numpy as np
import jax
import jax.numpy as jnp

def _softmax(x, axis=-1):
    return jax.nn.softmax(x, axis=axis)

def _gelu(x):
    return jax.nn.gelu(x, approximate=True)

def _silu(x):
    return jax.nn.silu(x)

def _sigmoid(x):
    return jax.nn.sigmoid(x)

def _layernorm(x, axis=-1, eps=1e-05):
    m = jnp.mean(x, axis=axis, keepdims=True)
    v = jnp.var(x, axis=axis, keepdims=True)
    return (x - m) / jnp.sqrt(v + eps)

def _scatter_add(tgt, idx, src, axis=0):
    return tgt.at[idx].add(src)

def _segment_sum(src, seg, n):
    return jax.ops.segment_sum(src, seg, n)
kernel_name = 'mk_xattn_ffn_d1_seqx_r2_7ed6f2'

def setup_inputs(seed: int=0):
    np.random.seed(seed)
    _w = jnp.asarray

    def _rec_inputs():
        import jax
        import jax.numpy as jnp
        _rk = jax.random.key(seed)
        x = -0.0002928 + 1 * jax.random.normal(jax.random.fold_in(_rk, 1), (16, 224, 512), jnp.float32)
        _lenS = 224 - jax.random.randint(jax.random.fold_in(_rk, 7), (16,), 0, max(1, 224 // 4) + 1, jnp.int32)
        _lenS2 = 750 - jax.random.randint(jax.random.fold_in(_rk, 8), (16,), 0, max(1, 750 // 4) + 1, jnp.int32)
        _ctx_1024P = jax.random.normal(jax.random.fold_in(_rk, 11), (16, 16, 512), jnp.float32)
        _ctx_1024c = jax.random.dirichlet(jax.random.fold_in(_rk, 511), 0.3 * jnp.ones((16,), jnp.float32), (16, 750))
        _ctx_1024t = jnp.einsum('bsk,bkd->bsd', _ctx_1024c, _ctx_1024P)
        _ctx_1024t = _ctx_1024t * jax.lax.rsqrt(jnp.mean(jnp.square(_ctx_1024t)) + 1e-12) * 0.953939
        ctx_1024 = -1.39393e-06 + 0.999914 * (_ctx_1024t + 0.3 * jax.random.normal(jax.random.fold_in(_rk, 611), (16, 750, 512), jnp.float32))
        return (x, ctx_1024)
    x, ctx_1024 = _rec_inputs()

    def _L0_xattn_setup():
        import jax, jax.numpy as jnp
        import numpy as np
        EMBED_DIM = 512
        NUM_HEADS = 16
        HEAD_DIM = EMBED_DIM // NUM_HEADS
        key = jax.random.key(seed)
        ks = jax.random.split(key, 7)
        B, S, E = (2, 1024, EMBED_DIM)
        bound = float(np.sqrt(6.0 / (E + E)))
        mkw = lambda k: jax.random.uniform(k, (E, E), jnp.float32, -bound, bound)
        return {'query': jax.random.normal(ks[0], (B, S, E), jnp.float32), 'key': jax.random.normal(ks[1], (B, S, E), jnp.float32), 'value': jax.random.normal(ks[2], (B, S, E), jnp.float32), 'Wq': mkw(ks[3]), 'Wk': mkw(ks[4]), 'Wv': mkw(ks[5]), 'Wo': mkw(ks[6])}
    _L0_xattn_all = _L0_xattn_setup()
    _L0_xattn_in = {k: v for k, v in _L0_xattn_all.items() if k in ('Wq', 'Wk', 'Wv', 'Wo')}
    del _L0_xattn_all

    def _L0_ffn_setup():
        import jax, jax.numpy as jnp
        import numpy as np
        HIDDEN = 512
        FF = 2048
        N_EXPERTS = 8
        CAP_FACTOR = 1.0
        B, S = (4, 1024)
        STD = 0.02

        def _gelu(x):
            return x * 0.5 * (1.0 + jax.lax.erf(x / 1.41421))
        key = jax.random.key(seed)
        ks = jax.random.split(key, 6)
        x = jax.random.normal(ks[0], (B, S, HIDDEN), dtype=jnp.float32)
        W_sw = jax.random.normal(ks[1], (HIDDEN, N_EXPERTS), dtype=jnp.float32) * STD
        b_sw = jnp.zeros((N_EXPERTS,), dtype=jnp.float32)
        W1 = jax.random.normal(ks[2], (N_EXPERTS, HIDDEN, FF), dtype=jnp.float32) * STD
        b1 = jnp.zeros((N_EXPERTS, FF), dtype=jnp.float32)
        W2 = jax.random.normal(ks[3], (N_EXPERTS, FF, HIDDEN), dtype=jnp.float32) * STD
        b2 = jnp.zeros((N_EXPERTS, HIDDEN), dtype=jnp.float32)
        return {'x': x, 'W_sw': W_sw, 'b_sw': b_sw, 'W1': W1, 'b1': b1, 'W2': W2, 'b2': b2}
    _L0_ffn_all = _L0_ffn_setup()
    _L0_ffn_in = {k: v for k, v in _L0_ffn_all.items() if k in ('W_sw', 'b_sw', 'W1', 'b1', 'W2', 'b2')}
    del _L0_ffn_all
    return {'x': x, 'ctx_1024': ctx_1024, 'L0_xattn_Wq': _L0_xattn_in['Wq'], 'L0_xattn_Wk': _L0_xattn_in['Wk'], 'L0_xattn_Wv': _L0_xattn_in['Wv'], 'L0_xattn_Wo': _L0_xattn_in['Wo'], 'L0_ffn_W_sw': _L0_ffn_in['W_sw'], 'L0_ffn_b_sw': _L0_ffn_in['b_sw'], 'L0_ffn_W1': _L0_ffn_in['W1'], 'L0_ffn_b1': _L0_ffn_in['b1'], 'L0_ffn_W2': _L0_ffn_in['W2'], 'L0_ffn_b2': _L0_ffn_in['b2']}

def reference(x, ctx_1024, L0_xattn_Wq, L0_xattn_Wk, L0_xattn_Wv, L0_xattn_Wo, L0_ffn_W_sw, L0_ffn_b_sw, L0_ffn_W1, L0_ffn_b1, L0_ffn_W2, L0_ffn_b2):
    import jax
    import jax.numpy as jnp

    def _L0_xattn_ref(query, key, value, Wq, Wk, Wv, Wo):
        import jax, jax.numpy as jnp
        import numpy as np
        EMBED_DIM = 512
        NUM_HEADS = 16
        HEAD_DIM = EMBED_DIM // NUM_HEADS
        B, L, E = query.shape
        H, D = (NUM_HEADS, HEAD_DIM)
        scale = D ** (-0.5)
        q = (query @ Wq.T).reshape(B, L, H, D) * scale
        k = (key @ Wk.T).reshape(B, -1, H, D)
        v = (value @ Wv.T).reshape(B, -1, H, D)
        scores = jax.nn.sigmoid(jnp.einsum('blhd,bshd->bhls', q, k))
        o = jnp.einsum('bhls,bshd->blhd', scores, v).reshape(B, L, E)
        return o @ Wo.T

    def _L0_ffn_ref(x, W_sw, b_sw, W1, b1, W2, b2):
        import jax, jax.numpy as jnp
        import numpy as np
        HIDDEN = 512
        FF = 2048
        N_EXPERTS = 8
        CAP_FACTOR = 1.0
        B, S = (4, 1024)
        STD = 0.02

        def _gelu(x):
            return x * 0.5 * (1.0 + jax.lax.erf(x / 1.41421))
        Bb, Ss, D = x.shape
        T = Bb * Ss
        E = W1.shape[0]
        capacity = int(CAP_FACTOR * T / E)
        xf = x.reshape(T, D)
        logits = xf @ W_sw + b_sw
        probs = jax.nn.softmax(logits, axis=-1)
        pmax = jnp.max(probs, axis=-1)
        routes = jnp.argmax(probs, axis=-1)
        factor = pmax / jax.lax.stop_gradient(pmax)
        xs = xf * factor[:, None]
        onehot = jax.nn.one_hot(routes, E, dtype=jnp.int32)
        pos = jnp.cumsum(onehot, axis=0) - 1
        pos_tok = jnp.take_along_axis(pos, routes[:, None], axis=1)[:, 0]
        keep = pos_tok < capacity
        pos_safe = jnp.where(keep, pos_tok, capacity)
        buf = jnp.zeros((E, capacity + 1, D), dtype=xs.dtype)
        buf = buf.at[routes, pos_safe].set(xs)
        buf = buf[:, :capacity]
        h = _gelu(jnp.einsum('ecd,edf->ecf', buf, W1) + b1[:, None, :])
        expert_out = jnp.einsum('ecf,efd->ecd', h, W2) + b2[:, None, :]
        gathered = expert_out[routes, jnp.minimum(pos_tok, capacity - 1)]
        final = jnp.where(keep[:, None], gathered, xs)
        return final.reshape(Bb, Ss, D)
    x = x + _L0_xattn_ref(_layernorm(x, axis=-1), ctx_1024, ctx_1024, L0_xattn_Wq, L0_xattn_Wk, L0_xattn_Wv, L0_xattn_Wo)
    x = x + _L0_ffn_ref(_layernorm(x, axis=-1), L0_ffn_W_sw, L0_ffn_b_sw, L0_ffn_W1, L0_ffn_b1, L0_ffn_W2, L0_ffn_b2)
    return x

_drawn_inputs = setup_inputs


def setup_inputs(seed=0):
    import zlib

    import numpy as np

    out = dict(_drawn_inputs(seed))
    spreads = {'L0_ffn_b_sw': (0.0, 0.8), 'L0_ffn_b1': (0.0, 2.0), 'L0_ffn_b2': (0.0, 2.0)}
    factors = {'L0_ffn_W_sw': 8.0, 'L0_ffn_W1': 8.0, 'L0_ffn_W2': 8.0}
    for name, (base, spread) in spreads.items():
        noise = np.random.default_rng([zlib.crc32(name.encode()), seed]).standard_normal(out[name].shape)
        drawn = base * np.exp(spread * noise) if base else spread * noise
        out[name] = jnp.asarray(drawn.astype(out[name].dtype))
    for name, factor in factors.items():
        out[name] = (out[name] * factor).astype(out[name].dtype)
    return out
```

```python
from contextlib import ExitStack

import concourse.bass as bass
from concourse import mybir

ALU = mybir.AluOpType
ACT = mybir.ActivationFunctionType
AX_X = mybir.AxisListType.X
F32 = mybir.dt.float32
F32R = mybir.dt.float32r
BF16 = mybir.dt.bfloat16
I32 = mybir.dt.int32
U32 = mybir.dt.uint32

P = 128
EPS = 1e-5
STRETCH = 2.0 ** 0.5 / 1.41421
NOWHERE = 65536.0

C_ID, C_LOW, C_ONE, C_BASE, C_RANK, C_TOK, C_END = 0, 128, 240, 352, 368, 384, 386


def hold(eng, sem, count):
    if not isinstance(count, int):
        count = eng.compute_val(count)
        eng.wait_ge(sem, 1)
    eng.wait_ge(sem, count)


def after(eng, sem, count):
    if isinstance(count, int) and count <= 0:
        return
    hold(eng, sem, count)


MID_LINKS = 37


class Links:

    def __init__(self, eng, sem):
        self.eng, self.sem, self.base, self.n = eng, sem, 0, 0

    def __call__(self, instruction):
        instruction.then_inc(self.sem, 1)
        self.n += 1

    def done(self):
        hold(self.eng, self.sem, self.base + self.n)


class Shapes:
    def __init__(self, x, ctx_t, w1, w2):
        self.B, self.L, self.D = x.shape
        self.S = ctx_t.shape[3]
        self.H, self.HD = 16, 32
        self.E, self.CH = w1.shape[0], w1.shape[1]
        self.FC = w1.shape[4]
        self.F = self.CH * self.FC
        self.T = self.B * self.L
        self.CAP = self.T // self.E
        self.TP = 112
        self.NT = self.L // self.TP
        self.KC = self.D // P
        self.SP = 125
        self.NS = self.S // self.SP
        self.G = self.H // 4
        self.HALF = self.S // 2
        self.ROW = 2 * self.D + 4


def attention_phase(nc, sh, x, ctx_t, wk_t, wv_t, wq_t, wo_t, w_sw, b_sw, consts, slots, out):
    B, L, D, S, KC, G, NS, TP, NT = sh.B, sh.L, sh.D, sh.S, sh.KC, sh.G, sh.NS, sh.TP, sh.NT
    SP, HALF, HD, ROW, E, CAP, T = sh.SP, sh.HALF, sh.HD, sh.ROW, sh.E, sh.CAP, sh.T
    NI = G * NS
    SCALE = float(HD) ** -0.5
    KQ = 12 * 16

    with ExitStack() as ctx:
        def sb(name, shape, dt=F32):
            return ctx.enter_context(nc.sbuf_tensor(name, shape, dt))

        def sem(name):
            return ctx.enter_context(nc.semaphore(name))

        ps_s = ctx.enter_context(nc.psum_tensor("ps_scores", [P, 2, 2, 512], F32))
        ps_o = ctx.enter_context(nc.psum_tensor("ps_o", [P, 512], F32))
        ps_a = ctx.enter_context(nc.psum_tensor("ps_a", [P, 512], F32))
        ps_b = ctx.enter_context(nc.psum_tensor("ps_b", [P, 512], F32))
        ps_c = ctx.enter_context(nc.psum_tensor("ps_c", [P, 512], F32))

        w_hl = {n: sb(f"w{n}_hl", [P, 2, KC, D], F32R) for n in "kvqo"}
        sw_raw = sb("sw_raw", [P, KC, E])
        sw_hl = sb("sw_hl", [P, KC, P], F32R)
        cst = sb("cst", [P, C_END])
        low16 = sb("low16", [TP, TP], BF16)
        one16 = sb("one16", [TP, TP], BF16)
        bsw = sb("bsw", [TP, NT, E])
        mhalf = sb("mhalf", [TP, NT])

        raw = sb("ctx_raw", [P, 2, S])
        ctx_hl = sb("ctx_hl", [P, 2, KC, S], F32R)
        v_sb = sb("v_sb", [P, NS, D])
        kq_hl = sb("kq_hl", [P, 2, 2, 4 * L], F32R)
        k_st = sb("k_st", [P, 2, 4, S], F32R)
        q_st = sb("q_st", [P, 4, G, L], F32R)
        probs = sb("probs", [P, 3, 4, L])
        tok_hl = sb("tok_hl", [P, 2, KC, L], F32R)
        o_hl = sb("o_hl", [P, 2, G, L], F32R)
        x_in = sb("x_in", [TP, NT, D])
        x_res = sb("x_res", [TP, NT, D])
        rows = sb("rows", [TP, NT, ROW])
        xn2 = sb("xn2", [TP, NT, D])
        st1 = sb("st1", [TP, NT, 6])
        st2 = sb("st2", [TP, NT, 6])
        mv1 = sb("mv1", [TP, NT, 2])
        mv2 = sb("mv2", [TP, NT, 2])
        var1 = sb("var1", [TP, NT])
        var2 = sb("var2", [TP, NT])
        rstd1 = sb("rstd1", [TP, NT])
        rstd2 = sb("rstd2", [TP, NT])
        lg0 = sb("lg0", [TP, NT, E])
        lg = sb("lg", [TP, NT, E])
        zed = sb("zed", [TP, NT, E])
        cand = sb("cand", [TP, NT, E])
        hot = sb("hot", [TP, NT, E])
        hot16 = sb("hot16", [TP, NT, E], BF16)
        sgp = sb("sgp", [TP, NT, E])
        sgn = sb("sgn", [TP, NT, E])
        prb = sb("prb", [TP, NT, E])
        posb = sb("posb", [TP, NT, E])
        eoff = sb("eoff", [TP, NT, E])
        cum = sb("cum", [TP, E])
        red = sb("red", [TP, 12, NT])
        slot_i = sb("slot_i", [TP, NT], I32)
        drop_i = sb("drop_i", [TP, NT], I32)

        cst_in = sem("cst_in")
        w_in = [sem(f"w_in{i}") for i in range(4)]
        raw_in = [sem("raw_in0"), sem("raw_in1")]
        x_in_s = sem("x_in_s")
        xres_in = sem("xres_in")
        kst_in = [sem("kst_in0"), sem("kst_in1")]
        qst_in = sem("qst_in")
        sent = sem("sent")
        k_proj, v_proj, q_proj = sem("k_proj"), sem("v_proj"), sem("q_proj")
        xn_turned, wo_out, x2_turned = sem("xn_turned"), sem("wo_out"), sem("x2_turned")
        logits_out, pos_out = sem("logits_out"), sem("pos_out")
        scores_out, pv_out = sem("scores_out"), sem("pv_out")
        w_hi, w_lo = sem("w_hi"), sem("w_lo")
        ctx_hi, ctx_lo = sem("ctx_hi"), sem("ctx_lo")
        k_hi, k_lo, q_hi, q_lo = sem("k_hi"), sem("k_lo"), sem("q_hi"), sem("q_lo")
        xnt_hi, xnt_lo, o_hi, o_lo = sem("xnt_hi"), sem("xnt_lo"), sem("o_hi"), sem("o_lo")
        x2t_hi, x2t_lo = sem("x2t_hi"), sem("x2t_lo")
        v_ready, probs_ready = sem("v_ready"), sem("probs_ready")
        router_sig = sem("router_sig")
        prep, mhalf_set = sem("prep"), sem("mhalf_set")
        cleared = sem("cleared")
        var1_ready, var2_ready = sem("var1_ready"), sem("var2_ready")
        rstd1_ready, rstd2_ready = sem("rstd1_ready"), sem("rstd2_ready")
        xn_ready, x2_ready, xn2_ready = sem("xn_ready"), sem("x2_ready"), sem("xn2_ready")
        z_ready, hot_ready, rows_ready = sem("z_ready"), sem("hot_ready"), sem("rows_ready")
        dve_link, pool_link = sem("dve_link"), sem("pool_link")

        ident = cst[0:TP, C_ID:C_ID + TP]
        three = ((0, 0), (0, 1), (1, 0))
        w_order = (("k", wk_t), ("v", wv_t), ("q", wq_t), ("o", wo_t))
        w_tmp = (v_sb[:, 0:4, :], probs[:, :, :, :].rearrange("p a h l -> p (a h l)")[:, 0:KC * D].rearrange("p (c d) -> p c d", d=D))

        def k_bank(g, h):
            return ((ps_a, ps_b), (ps_b, ps_c), (ps_b, ps_c), (ps_a, ps_b))[g][h]

        def v_bank(t):
            return (ps_c, ps_a, ps_b, ps_b, ps_c, ps_a)[t]

        def q_bank(i):
            return (ps_c, ps_a)[i]

        def x_rows(b):
            return x[b].rearrange("(i p) d -> p i d", p=TP)

        block = ctx.enter_context(nc.Block())

        @block.sync
        def _(sp):
            sp.dma_start(w_tmp[0], wk_t).then_inc(w_in[0], 16)
            sp.dma_start(raw[:, 0, :], ctx_t[0, 0]).then_inc(raw_in[0], 16)
            sp.dma_start(raw[:, 1, :], ctx_t[0, 1]).then_inc(raw_in[1], 16)
            sp.dma_start(x_in[:], x_rows(0)).then_inc(x_in_s, 16)
            sp.dma_start(cst[:], consts).then_inc(cst_in, 16)
            sp.dma_start(w_tmp[1], wv_t).then_inc(w_in[1], 16)
            sp.dma_start(sw_raw[:], w_sw).then_inc(cst_in, 16)
            sp.dma_start(bsw[:], b_sw.partition_broadcast(TP)[:, None, :].broadcast_to([TP, NT, E])).then_inc(cst_in, 16)
            for k in (2, 3):
                hold(sp, ctx_lo, k - 1)
                sp.dma_start(raw[:, k % 2, :], ctx_t[0, k]).then_inc(raw_in[k % 2], 16)
            for n in (2, 3):
                hold(sp, w_lo, n - 1)
                sp.dma_start(w_tmp[n % 2], w_order[n][1]).then_inc(w_in[n], 16)

            def stack_k(b, g):
                hold(sp, k_lo, 8 * b + 2 * g + 2)
                after(sp, scores_out, NI * b + NS * (g - 1))
                for j in range(4):
                    for s, part in enumerate((0, 0, 1)):
                        sp.dma_start(k_st[32 * s:32 * s + 32, g % 2, j, :].bitcast(F32),
                                     kq_hl[32 * j:32 * j + 32, g % 2, part, 0:S].bitcast(F32)).then_inc(kst_in[g % 2], 16)

            def stack_q(b):
                hold(sp, q_lo, 2 * b + 2)
                after(sp, scores_out, NI * b)
                for j in range(4):
                    for s, part in enumerate((0, 1, 0)):
                        sp.dma_start(q_st[32 * s:32 * s + 32, j, :, :].rearrange("p g l -> p (g l)").bitcast(F32),
                                     kq_hl[32 * j:32 * j + 32, 0, part, :].bitcast(F32)).then_inc(qst_in, 16)

            def body(b, last=False, first=False):
                if not last:
                    for k in (0, 1):
                        hold(sp, ctx_lo, 4 * b + k + 3)
                        sp.dma_start(raw[:, k, :], ctx_t[b + 1, k]).then_inc(raw_in[k], 16)
                stack_k(b, 0)
                stack_k(b, 1)
                if not last:
                    hold(sp, xn_turned, 2 * b + 2)
                    sp.dma_start(x_in[:], x_rows(b + 1)).then_inc(x_in_s, 16)
                stack_q(b)
                stack_k(b, 2)
                stack_k(b, 3)
                if not last:
                    for k in (2, 3):
                        hold(sp, ctx_lo, 4 * b + k + 3)
                        sp.dma_start(raw[:, k - 2, :], ctx_t[b + 1, k]).then_inc(raw_in[k - 2], 16)
                if not first:
                    hold(sp, x2_ready, 2 * b)
                sp.dma_start(x_res[:], x_rows(b)).then_inc(xres_in, 16)

            body(0, first=True)
            with sp.Fori(1, B - 1) as b:
                body(b)
            body(B - 1, last=True)

        @block.gpsimd
        def _(pool):
            link = Links(pool, pool_link)
            nc.gpsimd.memset(mhalf[:], -0.5).then_inc(mhalf_set, 1)

            def split_hi(b):
                for k in range(KC):
                    hold(pool, raw_in[k % 2], 16 * (2 * b + k // 2 + 1))
                    if k == 0:
                        after(pool, k_proj, 8 * b)
                    nc.gpsimd.tensor_copy(ctx_hl[:, 0, k, :], raw[:, k % 2, :]).then_inc(ctx_hi, 1)

            def inverse_std(ready, done, mv, var, rstd, n):
                hold(pool, ready, n + 1)
                link(nc.gpsimd.tensor_scalar(var[:], mv[:, :, 1], EPS, None, ALU.add))
                link.done()
                nc.gpsimd.tensor_tensor(rstd[:], var[:], mhalf[:], ALU.pow).then_inc(done, 1)

            def scatter(r):
                hold(pool, rows_ready, r + 1)
                for i in range(NT):
                    nc.gpsimd.indirect_dma_start(
                        out=slots, out_offset=bass.IndirectOffsetOnAxis(ap=slot_i[:, i:i + 1].bitcast(U32), axis=0),
                        in_=rows[:, i, :], in_offset=None, bounds_check=T - 1, oob_is_err=False).then_inc(sent, 16)
                for i in range(NT):
                    nc.gpsimd.indirect_dma_start(
                        out=out, out_offset=bass.IndirectOffsetOnAxis(ap=drop_i[:, i:i + 1].bitcast(U32), axis=0),
                        in_=xn2[:, i, :], in_offset=None, bounds_check=T - 1, oob_is_err=False).then_inc(sent, 16)

            split_hi(0)
            hold(pool, mhalf_set, 1)
            inverse_std(var1_ready, rstd1_ready, mv1, var1, rstd1, 0)
            hold(pool, cleared, 2)
            n = T // TP // 4
            for q in range(4):
                dst = slots[q * n * TP:(q + 1) * n * TP, :].rearrange("(i p) c -> p i c", p=TP)
                pool.dma_start(dst, rows[:, 0:1, :].broadcast_to([TP, n, ROW])).then_inc(sent, 16)

            def body(b, first=False, last=False):
                if not first:
                    inverse_std(var2_ready, rstd2_ready, mv2, var2, rstd2, b - 1)
                if not last:
                    split_hi(b + 1)
                    inverse_std(var1_ready, rstd1_ready, mv1, var1, rstd1, b + 1)
                if not first:
                    scatter(b - 1)

            body(0, first=True)
            assert link.n == 2
            with pool.Fori(1, B - 1) as b:
                link.base, link.n = 2 * b, 0
                body(b)
            link.base, link.n = 2 * (B - 1), 0
            body(B - 1, last=True)
            inverse_std(var2_ready, rstd2_ready, mv2, var2, rstd2, B - 1)
            scatter(B - 1)
            hold(pool, sent, 64 * (B + 1))

        @block.scalar
        def _(act):
            for n, (name, _) in enumerate(w_order):
                act.wait_ge(w_in[n], 16)
                nc.scalar.copy(w_hl[name][:, 0], w_tmp[n % 2]).then_inc(w_hi, 1)

            def k_split(b, g, h):
                if h == 0:
                    after(act, kst_in[g % 2], KQ * (2 * b + g // 2))
                    if g == 2:
                        act.wait_ge(qst_in, KQ * (b + 1))
                act.wait_ge(k_proj, 8 * b + 2 * g + h + 1)
                bank = k_bank(g, h)
                nc.scalar.copy(kq_hl[:, g % 2, 0, h * HALF:(h + 1) * HALF], bank[:, h:h + HALF]).then_inc(k_hi, 1)

            def turned(b, i, source, done, sem_in):
                act.wait_ge(sem_in, 2 * b + i + 1)
                dst = tok_hl[:, 0, :, i * TP:(i + 1) * TP]
                nc.scalar.copy(dst, source[:, 0:KC * TP].rearrange("p (c t) -> p c t", t=TP)).then_inc(done, 1)

            def values(b, t):
                act.wait_ge(v_proj, NS * b + t + 1)
                if isinstance(b, int) and b == 0 and t < 4:
                    act.wait_ge(w_lo, 3)
                nc.scalar.copy(v_sb[0:SP, t, :], v_bank(t)[0:SP, :]).then_inc(v_ready, 1)

            def queries(b, i):
                act.wait_ge(q_proj, 2 * b + i + 1)
                if i == 0:
                    act.wait_ge(kst_in[0], KQ * (2 * b + 1))
                nc.scalar.activation(kq_hl[:, 0, 0, 2 * L * i:2 * L * (i + 1)], q_bank(i)[:, 0:2 * L],
                                     ACT.Copy, scale=SCALE).then_inc(q_hi, 1)

            def sigmoid(b, i):
                act.wait_ge(scores_out, NI * b + i + 1)
                nc.scalar.activation(probs[0:SP, i % 3].rearrange("p (a h) l -> p a (h l)", a=2),
                                     ps_s[0:SP, i % 2, :, 0:2 * L], ACT.Sigmoid).then_inc(probs_ready, 1)

            def attended(b, g):
                act.wait_ge(pv_out, NI * b + NS * (g + 1))
                nc.scalar.copy(o_hl[:, 0, g, :], ps_o[:, 0:L]).then_inc(o_hi, 1)

            def router(r):
                act.wait_ge(z_ready, r + 1)
                nc.scalar.activation(sgp[:], zed[:], ACT.Sigmoid).then_inc(router_sig, 1)
                nc.scalar.activation(sgn[:], zed[:], ACT.Sigmoid, scale=-1.0).then_inc(router_sig, 1)

            def body(b, first=False):
                for g in (0, 1):
                    k_split(b, g, 0)
                    k_split(b, g, 1)
                turned(b, 0, ps_a, xnt_hi, xn_turned)
                turned(b, 1, ps_b, xnt_hi, xn_turned)
                for t in (0, 1, 2):
                    values(b, t)
                queries(b, 0)
                queries(b, 1)
                for t in (3, 4, 5):
                    values(b, t)
                if first:
                    act.wait_ge(w_lo, 4)
                for i in range(NI):
                    sigmoid(b, i)
                    if i in (2, 5, 8, 11):
                        k_split(b, 2 + i // 6, (i // 3) % 2)
                    if i in (7, 13, 19):
                        attended(b, i // 6 - 1)
                    if not first and i in (14, 16):
                        turned(b - 1, i // 16, (ps_c, ps_a)[i // 16], x2t_hi, x2_turned)
                    if not first and i == 20:
                        router(b - 1)
                attended(b, G - 1)

            body(0, first=True)
            with act.Fori(1, B) as b:
                body(b)
            turned(B - 1, 0, ps_b, x2t_hi, x2_turned)
            turned(B - 1, 1, ps_c, x2t_hi, x2_turned)
            router(B - 1)

        @block.vector
        def _(dve):
            v = nc.vector
            link = Links(dve, dve_link)

            def less(dst, whole, hi, scale=None):
                if scale is None:
                    return v.tensor_tensor(dst, whole, hi.bitcast(F32), ALU.subtract)
                return v.scalar_tensor_tensor(out=dst, in0=whole, scalar=scale, in1=hi.bitcast(F32),
                                              op0=ALU.mult, op1=ALU.subtract)

            v.memset(rows[:, 0, 0:2 * D], 0.0).then_inc(cleared, 1)
            v.memset(rows[:, 0, 2 * D:ROW].bitcast(I32), int(NOWHERE)).then_inc(cleared, 1)
            v.memset(cum[:], 0.0).then_inc(prep, 1)
            v.memset(rows[:, 1, 2 * D:ROW].bitcast(I32), 0).then_inc(prep, 1)

            def split_lo(b):
                for k in range(KC):
                    dve.wait_ge(ctx_hi, 4 * b + k + 1)
                    less(ctx_hl[:, 1, k, :], raw[:, k % 2, :], ctx_hl[:, 0, k, :]).then_inc(ctx_lo, 1)

            def norm_stats(src, st, mv, ready, waits=()):
                for s, c in waits:
                    after(dve, s, c)
                for i in range(NT):
                    link(v.bn_stats(st[:, i, :], src(i)))
                link.done()
                for i in range(NT):
                    ins = v.bn_aggr(mv[:, i, :], st[:, i, :])
                    if i < NT - 1:
                        link(ins)
                    else:
                        ins.then_inc(ready, 1)

            def norm1(b):
                norm_stats(lambda i: x_in[:, i, :], st1, mv1, var1_ready, ((x_in_s, 16 * (b + 1)),))
                dve.wait_ge(rstd1_ready, b + 1)
                for i in range(NT):
                    v.tensor_scalar(x_in[:, i, :], x_in[:, i, :], mv1[:, i, 0:1], rstd1[:, i:i + 1],
                                    ALU.subtract, ALU.mult).then_inc(xn_ready, 1)

            def k_split(b, g, h):
                dve.wait_ge(k_hi, 8 * b + 2 * g + h + 1)
                cols = slice(h * HALF, (h + 1) * HALF)
                less(kq_hl[:, g % 2, 1, cols], k_bank(g, h)[:, h:h + HALF],
                     kq_hl[:, g % 2, 0, cols]).then_inc(k_lo, 1)

            def turned(b, i, source, ready, done):
                dve.wait_ge(ready, 2 * b + i + 1)
                cols = slice(i * TP, (i + 1) * TP)
                less(tok_hl[:, 1, :, cols], source[:, 0:KC * TP].rearrange("p (c t) -> p c t", t=TP),
                     tok_hl[:, 0, :, cols]).then_inc(done, 1)

            def queries(b, i):
                dve.wait_ge(q_hi, 2 * b + i + 1)
                cols = slice(2 * L * i, 2 * L * (i + 1))
                less(kq_hl[:, 0, 1, cols], q_bank(i)[:, 0:2 * L], kq_hl[:, 0, 0, cols], SCALE).then_inc(q_lo, 1)

            def attended(b, g):
                dve.wait_ge(o_hi, G * b + g + 1)
                less(o_hl[:, 1, g, :], ps_o[:, 0:L], o_hl[:, 0, g, :]).then_inc(o_lo, 1)

            def residual(r, i):
                if i == 0:
                    dve.wait_ge(sent, 64 * (r + 1))
                    dve.wait_ge(xres_in, 16 * (r + 1))
                dve.wait_ge(wo_out, 2 * r + i + 1)
                v.tensor_tensor(rows[:, i, D:2 * D], (ps_c, ps_a)[i][0:TP, 0:D], x_res[:, i, :],
                                ALU.add).then_inc(x2_ready, 1)

            def norm2_stats(r):
                norm_stats(lambda i: rows[:, i, D:2 * D], st2, mv2, var2_ready, ((x2_ready, 2 * r + 2),))

            def norm2(r):
                dve.wait_ge(rstd2_ready, r + 1)
                for i in range(NT):
                    v.tensor_scalar(xn2[:, i, :], rows[:, i, D:2 * D], mv2[:, i, 0:1], rstd2[:, i:i + 1],
                                    ALU.subtract, ALU.mult).then_inc(xn2_ready, 1)

            def wide(t, n=E):
                return t[:, :, None].broadcast_to([TP, NT, n])

            mx, best, tot, rtot, pmax, rpmax, factor, pos, eslot, kept, place, spare = (red[:, n, :] for n in range(12))
            base = cst[0:TP, C_BASE:C_BASE + NT * E].rearrange("p (i e) -> p i e", e=E)
            rank = cst[0:TP, C_RANK:C_RANK + NT * E].rearrange("p (i e) -> p i e", e=E)
            token = cst[0:TP, C_TOK:C_TOK + NT]

            def choose(r, bank):
                dve.wait_ge(logits_out, r + 1)
                lo = bank[0:TP, 0:NT * P].rearrange("p (i n) -> p i n", n=P)
                link(v.tensor_tensor(lg0[:], lo[:, :, 0:E], bsw[:], ALU.add))
                link.done()
                link(v.tensor_tensor(lg[:], lo[:, :, E:2 * E], lg0[:], ALU.add))
                link.done()
                link(v.tensor_reduce(mx, lg[:], AX_X, ALU.max))
                link.done()
                v.tensor_tensor(zed[:], lg[:], wide(mx), ALU.subtract).then_inc(z_ready, 1)
                link(v.tensor_tensor(cand[:], lg[:], wide(mx), ALU.is_equal))
                link.done()
                link(v.tensor_tensor(cand[:], cand[:], rank, ALU.mult))
                link.done()
                link(v.tensor_reduce(best, cand[:], AX_X, ALU.max))
                link.done()
                v.tensor_tensor(hot16[:], cand[:], wide(best), ALU.is_equal).then_inc(hot_ready, 1)
                link(v.tensor_tensor(hot[:], cand[:], wide(best), ALU.is_equal))

            def scale_tokens(r):
                dve.wait_ge(router_sig, 2 * r + 2)
                link(v.reciprocal(sgn[:], sgn[:]))
                link.done()
                link(v.tensor_tensor(prb[:], sgp[:], sgn[:], ALU.mult))
                link.done()
                link(v.tensor_reduce(tot, prb[:], AX_X, ALU.add))
                link.done()
                link(v.reciprocal(rtot, tot))
                link.done()
                link(v.tensor_tensor(prb[:], prb[:], wide(rtot), ALU.mult))
                link.done()
                link(v.tensor_reduce(pmax, prb[:], AX_X, ALU.max))
                link.done()
                link(v.reciprocal(rpmax, pmax))
                link.done()
                link(v.tensor_tensor(factor, pmax, rpmax, ALU.mult))
                link.done()
                for i in range(NT):
                    link(v.tensor_scalar(rows[:, i, 0:D], xn2[:, i, :], factor[:, i:i + 1], None, ALU.mult))

            def place_tokens(r, bank):
                dve.wait_ge(pos_out, r + 1)
                link.done()
                before = bank[0:TP, 0:NT * E].rearrange("p (i e) -> p i e", e=E)
                link(v.tensor_tensor(posb[:], before, cum[:, None, :].broadcast_to([TP, NT, E]), ALU.add))
                link(v.tensor_tensor(eoff[:], hot[:], base, ALU.mult))
                link.done()
                link(v.tensor_tensor(cum[:], bank[0:TP, NT * E:(NT + 1) * E], cum[:], ALU.add))
                link(v.tensor_tensor(posb[:], posb[:], hot[:], ALU.mult))
                link(v.tensor_reduce(eslot, eoff[:], AX_X, ALU.add))
                link.done()
                link(v.tensor_reduce(pos, posb[:], AX_X, ALU.add))
                link.done()
                link(v.tensor_scalar(spare, pos, float(CAP), NOWHERE, ALU.is_ge, ALU.mult))
                link(v.tensor_scalar(kept, pos, float(CAP), NOWHERE, ALU.is_lt, ALU.mult))
                link(v.tensor_tensor(place, pos, eslot, ALU.add))
                link.done()
                link(v.tensor_tensor(slot_i[:], place, spare, ALU.add))
                link(v.tensor_tensor(drop_i[:], token, kept, ALU.add))
                link(v.tensor_copy(rows[:, :, 2 * D].bitcast(I32), token))
                link(v.tensor_scalar(token, token, float(L), None, ALU.add))
                link(v.tensor_tensor(xn2[:, 0, :], rows[:, 0, 0:D], rows[:, 0, D:2 * D], ALU.add))
                link.done()
                v.tensor_tensor(xn2[:, 1, :], rows[:, 1, 0:D], rows[:, 1, D:2 * D], ALU.add).then_inc(rows_ready, 1)

            split_lo(0)
            dve.wait_ge(w_hi, 1)
            less(w_hl["k"][:, 1], w_tmp[0], w_hl["k"][:, 0]).then_inc(w_lo, 1)
            norm1(0)
            for n in (1, 2, 3):
                name = w_order[n][0]
                dve.wait_ge(w_hi, n + 1)
                less(w_hl[name][:, 1], w_tmp[n % 2], w_hl[name][:, 0]).then_inc(w_lo, 1)
            dve.wait_ge(cst_in, 48)
            v.memset(sw_hl[:].bitcast(I32), 0).then_inc(prep, 1)
            dve.wait_ge(prep, 3)
            v.tensor_copy(sw_hl[:, :, 0:E], sw_raw[:]).then_inc(prep, 1)
            dve.wait_ge(prep, 4)
            less(sw_hl[:, :, E:2 * E], sw_raw[:], sw_hl[:, :, 0:E]).then_inc(prep, 1)
            v.tensor_copy(low16[:], cst[0:TP, C_LOW:C_LOW + TP]).then_inc(prep, 1)
            v.tensor_copy(one16[:], cst[0:TP, C_ONE:C_ONE + TP]).then_inc(prep, 1)

            def body(b, first=False, last=False):
                k_split(b, 0, 0)
                k_split(b, 0, 1)
                if not first:
                    residual(b - 1, 0)
                    residual(b - 1, 1)
                k_split(b, 1, 0)
                k_split(b, 1, 1)
                turned(b, 0, ps_a, xnt_hi, xnt_lo)
                turned(b, 1, ps_b, xnt_hi, xnt_lo)
                if not first:
                    norm2_stats(b - 1)
                queries(b, 0)
                queries(b, 1)
                if not first:
                    norm2(b - 1)
                k_split(b, 2, 0)
                k_split(b, 2, 1)
                attended(b, 0)
                k_split(b, 3, 0)
                k_split(b, 3, 1)
                attended(b, 1)
                if not first:
                    turned(b - 1, 0, ps_c, x2t_hi, x2t_lo)
                    turned(b - 1, 1, ps_a, x2t_hi, x2t_lo)
                if not last:
                    split_lo(b + 1)
                if not first:
                    choose(b - 1, ps_b)
                attended(b, 2)
                if not first:
                    scale_tokens(b - 1)
                if not last:
                    norm1(b + 1)
                if not first:
                    place_tokens(b - 1, ps_c)
                attended(b, 3)

            links = []
            links.append(link.n)
            body(0, first=True)
            start = link.n
            with dve.Fori(1, B - 1) as b:
                link.base, link.n = start + MID_LINKS * (b - 1), 0
                body(b)
                assert link.n == MID_LINKS, link.n
            link.base, link.n = start + MID_LINKS * (B - 2), 0
            body(B - 1, last=True)
            residual(B - 1, 0)
            residual(B - 1, 1)
            norm2_stats(B - 1)
            norm2(B - 1)
            turned(B - 1, 0, ps_b, x2t_hi, x2t_lo)
            turned(B - 1, 1, ps_c, x2t_hi, x2t_lo)
            choose(B - 1, ps_a)
            scale_tokens(B - 1)
            place_tokens(B - 1, ps_b)

        @block.tensor
        def _(pe):
            mm = nc.tensor.matmul

            def project_k(b, g, h, part=None):
                bank = k_bank(g, h)
                chunks = range(KC) if part is None else ((0,), (1, 2), (3,))[part]
                for k in chunks:
                    if g == 0 and h == 0:
                        pe.wait_ge(ctx_lo, 4 * b + k + 1)
                    for n, (a, c) in enumerate(three):
                        last = mm(bank[:, 0:HALF + 1], w_hl["k"][:, a, k, g * P:(g + 1) * P],
                                  ctx_hl[:, c, k, h * (HALF - 1):h * (HALF - 1) + HALF + 1],
                                  start=(k == 0 and n == 0), stop=(k == KC - 1 and n == 2))
                if part in (None, 2):
                    last.then_inc(k_proj, 1)

            def project_v(b, t):
                for k in range(KC):
                    for n, (a, c) in enumerate(three):
                        last = mm(v_bank(t)[0:SP, :], ctx_hl[:, a, k, t * SP:(t + 1) * SP], w_hl["v"][:, c, k, :],
                                  start=(k == 0 and n == 0), stop=(k == KC - 1 and n == 2))
                last.then_inc(v_proj, 1)

            def project_q(b, i):
                for g in (2 * i, 2 * i + 1):
                    for k in range(KC):
                        for n, (a, c) in enumerate(three):
                            last = mm(q_bank(i)[:, (g % 2) * L:(g % 2 + 1) * L], w_hl["q"][:, a, k, g * P:(g + 1) * P],
                                      tok_hl[:, c, k, :], start=(k == 0 and n == 0), stop=(k == KC - 1 and n == 2))
                last.then_inc(q_proj, 1)

            def project_o(r, i, bank):
                for g in range(G):
                    for n, (a, c) in enumerate(three):
                        last = mm(bank[0:TP, :], o_hl[:, a, g, i * TP:(i + 1) * TP], w_hl["o"][:, c, g, :],
                                  start=(g == 0 and n == 0), stop=(g == G - 1 and n == 2))
                last.then_inc(wo_out, 1)

            def turn(src, i, bank, done):
                for k in range(KC):
                    last = nc.tensor.transpose(bank[:, k * TP:(k + 1) * TP], src[:, i, k * P:(k + 1) * P], ident)
                last.then_inc(done, 1)

            def scores(b, i):
                g, t = divmod(i, NS)
                if t == 0:
                    pe.wait_ge(kst_in[g % 2], KQ * (2 * b + g // 2 + 1))
                if i == 0:
                    pe.wait_ge(qst_in, KQ * (b + 1))
                after(pe, probs_ready, NI * b + i - 1)
                for j in range(4):
                    last = mm(ps_s[0:SP, i % 2, j // 2, (j % 2) * L:(j % 2 + 1) * L],
                              k_st[0:96, g % 2, j, t * SP:(t + 1) * SP], q_st[0:96, j, g, :],
                              start=True, stop=True)
                last.then_inc(scores_out, 1)

            def attend(b, i):
                g, t = divmod(i, NS)
                if i == 0:
                    pe.wait_ge(v_ready, NS * (b + 1))
                if t == 0:
                    after(pe, o_lo, G * b + g)
                pe.wait_ge(probs_ready, NI * b + i + 1)
                for j in range(4):
                    h = 4 * g + j
                    last = mm(ps_o[HD * j:HD * (j + 1), 0:L], v_sb[0:SP, t, HD * h:HD * (h + 1)],
                              probs[0:SP, i % 3, j, :], start=(t == 0), stop=(t == NS - 1))
                last.then_inc(pv_out, 1)

            def route(r, bank):
                pe.wait_ge(x2t_lo, 2 * r + 2)
                for i in range(NT):
                    for k in range(KC):
                        for a in (0, 1):
                            last = mm(bank[0:TP, i * P:(i + 1) * P], tok_hl[:, a, k, i * TP:(i + 1) * TP],
                                      sw_hl[:, k, :], start=(k == 0 and a == 0), stop=(k == KC - 1 and a == 1))
                last.then_inc(logits_out, 1)

            def count(r, bank):
                pe.wait_ge(hot_ready, r + 1)
                mm(bank[0:TP, 0:E], low16[:], hot16[:, 0, :], start=True, stop=True)
                mm(bank[0:TP, E:2 * E], low16[:], hot16[:, 1, :], start=True, stop=False)
                mm(bank[0:TP, E:2 * E], one16[:], hot16[:, 0, :], start=False, stop=True)
                mm(bank[0:TP, 2 * E:3 * E], one16[:], hot16[:, 0, :], start=True, stop=False)
                mm(bank[0:TP, 2 * E:3 * E], one16[:], hot16[:, 1, :], start=False, stop=True).then_inc(pos_out, 1)

            def body(b, first=False):
                if first:
                    pe.wait_ge(w_lo, 1)
                project_k(b, 0, 0)
                project_k(b, 0, 1)
                if not first:
                    pe.wait_ge(o_lo, G * b)
                    project_o(b - 1, 0, ps_c)
                    pe.wait_ge(k_lo, 8 * b + 1)
                    project_o(b - 1, 1, ps_a)
                pe.wait_ge(k_lo, 8 * b + 2)
                project_k(b, 1, 0)
                if not first:
                    pe.wait_ge(x2_ready, 2 * b - 1)
                project_k(b, 1, 1)
                if first:
                    pe.wait_ge(k_lo, 1)
                    pe.wait_ge(cst_in, 48)
                else:
                    pe.wait_ge(x2_ready, 2 * b)
                pe.wait_ge(xn_ready, 2 * b + 1)
                turn(x_in, 0, ps_a, xn_turned)
                pe.wait_ge(k_lo, 8 * b + 3)
                pe.wait_ge(xn_ready, 2 * b + 2)
                turn(x_in, 1, ps_b, xn_turned)
                if first:
                    pe.wait_ge(w_lo, 2)
                pe.wait_ge(k_lo, 8 * b + 4)
                project_v(b, 0)
                pe.wait_ge(xnt_lo, 2 * b + 1)
                project_v(b, 1)
                pe.wait_ge(xnt_lo, 2 * b + 2)
                project_v(b, 2)
                if first:
                    pe.wait_ge(w_lo, 3)
                pe.wait_ge(v_ready, NS * b + 1)
                project_q(b, 0)
                pe.wait_ge(v_ready, NS * b + 2)
                project_q(b, 1)
                pe.wait_ge(v_ready, NS * b + 3)
                project_v(b, 3)
                pe.wait_ge(q_lo, 2 * b + 1)
                project_v(b, 4)
                pe.wait_ge(q_lo, 2 * b + 2)
                project_v(b, 5)
                for i in range(NI):
                    scores(b, i)
                    if i < 12:
                        if i == 0:
                            pe.wait_ge(v_ready, NS * b + 4)
                        if i == 3:
                            pe.wait_ge(v_ready, NS * b + 5)
                        if i == 6:
                            pe.wait_ge(v_ready, NS * b + 6)
                        if i == 9:
                            pe.wait_ge(k_lo, 8 * b + 5)
                        project_k(b, 2 + i // 6, (i // 3) % 2, i % 3)
                    if not first:
                        if i == 14:
                            pe.wait_ge(k_lo, 8 * b + 6)
                            pe.wait_ge(xn2_ready, 2 * b - 1)
                            turn(xn2, 0, ps_c, x2_turned)
                        if i == 16:
                            pe.wait_ge(k_lo, 8 * b + 7)
                            pe.wait_ge(xn2_ready, 2 * b)
                            turn(xn2, 1, ps_a, x2_turned)
                        if i == 17:
                            pe.wait_ge(k_lo, 8 * b + 8)
                            route(b - 1, ps_b)
                        if i == 22:
                            count(b - 1, ps_c)
                    if i >= 2:
                        attend(b, i - 2)
                attend(b, NI - 2)
                attend(b, NI - 1)

            body(0, first=True)
            pe.wait_ge(w_lo, 4)
            pe.wait_ge(prep, 7)
            with pe.Fori(1, B) as b:
                body(b)
            r = B - 1
            pe.wait_ge(o_lo, G * B)
            project_o(r, 0, ps_c)
            project_o(r, 1, ps_a)
            pe.wait_ge(xn2_ready, 2 * r + 1)
            turn(xn2, 0, ps_b, x2_turned)
            pe.wait_ge(xn2_ready, 2 * r + 2)
            turn(xn2, 1, ps_c, x2_turned)
            route(r, ps_a)
            count(r, ps_b)



def expert_phase(nc, sh, w1, w2, b1, b2, consts, slots, out):
    D, KC, TP, ROW, E, CAP, T, CH, FC = sh.D, sh.KC, sh.TP, sh.ROW, sh.E, sh.CAP, sh.T, sh.CH, sh.FC
    NST = CAP // TP
    NF = FC // P
    FT = CH * NF

    with ExitStack() as ctx:
        def sb(name, shape, dt=F32):
            return ctx.enter_context(nc.sbuf_tensor(name, shape, dt))

        def sem(name):
            return ctx.enter_context(nc.semaphore(name))

        ps_y = ctx.enter_context(nc.psum_tensor("ps_y", [P, 4, 512], F32))
        ps_h = ctx.enter_context(nc.psum_tensor("ps_h", [P, 4, 512], F32))

        idt = sb("idt", [TP, TP])
        b1_sb = sb("b1_sb", [P, E, FT])
        b1s = sb("b1s", [P, E, FT])
        b2_sb = sb("b2_sb", [TP, 2, D])
        xs_in = sb("xs_in", [TP, NST, D])
        res = sb("res", [TP, NST, D + 4])
        res_b = sb("res_b", [TP, NST, D])
        tok = sb("tok", [TP, NST], I32)
        xs_hl = sb("xs_hl", [P, 2, KC, CAP], F32R)
        w1_raw = sb("w1_raw", [P, 4, KC, FC])
        w2_raw = sb("w2_raw", [P, 4, NF, D])
        w1_hl = sb("w1_hl", [P, 2, 2, KC, FC], F32R)
        w2_hl = sb("w2_hl", [P, 2, 2, NF, D], F32R)
        hid = sb("hid", [P, 2, CAP])
        hid_hl = sb("hid_hl", [P, 4, 2, CAP], F32R)
        y_sb = sb("y_sb", [TP, NST, D])

        cst_in = sem("cst_in2")
        xs_in_s, res_in, b2_in = sem("xs_in_s"), sem("res_in"), sem("b2_in")
        w1_in = [sem(f"w1_in{i}") for i in range(4)]
        w2_in = [sem(f"w2_in{i}") for i in range(4)]
        stored = sem("stored")
        b1_scaled = sem("b1_scaled")
        xs_turned, xs_hi, xs_lo = sem("xs_turned"), sem("xs_hi"), sem("xs_lo")
        w1_hi, w1_lo, w2_hi, w2_lo = sem("w1_hi"), sem("w1_lo"), sem("w2_hi"), sem("w2_lo")
        h_out, gelu_done, h_hi, h_lo = sem("h_out"), sem("gelu_done"), sem("h_hi"), sem("h_lo")
        y_chunk, y_ready = sem("y_chunk"), sem("y_ready")
        res_ready = sem("res_ready")

        three = ((0, 0), (0, 1), (1, 0))

        block = ctx.enter_context(nc.Block())

        def slot_rows(e):
            return slots.rearrange("(e i p) c -> e p i c", e=E, p=TP)[e]

        @block.sync
        def _(sp):
            def load_chunk(e, c):
                if not (isinstance(e, int) and e == 0 and c < 4):
                    hold(sp, w1_lo, CH * e + c - 3)
                    hold(sp, w2_lo, CH * e + c - 3)
                sp.dma_start(w1_raw[:, c % 4], w1[e, c]).then_inc(w1_in[c % 4], 16)
                sp.dma_start(w2_raw[:, c % 4], w2[e, c]).then_inc(w2_in[c % 4], 16)

            def load_slots(e):
                after(sp, xs_turned, KC * e)
                sp.dma_start(xs_in[:], slot_rows(e)[:, :, 0:D]).then_inc(xs_in_s, 16)

            def load_residual(e):
                after(sp, res_ready, 2 * e)
                sp.dma_start(res[:], slot_rows(e)[:, :, D:ROW]).then_inc(res_in, 16)
                sp.dma_start(b2_sb[:, 0, :], b2[e].partition_broadcast(TP)).then_inc(b2_in, 16)

            load_slots(0)
            sp.dma_start(idt[:], consts[0:TP, C_ID:C_ID + TP]).then_inc(cst_in, 16)
            sp.dma_start(b1_sb[:], b1).then_inc(cst_in, 16)
            for c in range(4):
                load_chunk(0, c)
            load_residual(0)

            def body(e, last=False):
                for c in range(4, CH):
                    load_chunk(e, c)
                    if c == 5 and not last:
                        load_slots(e + 1)
                if not last:
                    for c in range(4):
                        load_chunk(e + 1, c)
                    load_residual(e + 1)

            with sp.Fori(0, E - 1) as e:
                body(e)
            body(E - 1, last=True)

        @block.gpsimd
        def _(pool):
            def split_w2(e, c):
                hold(pool, w2_in[c % 4], 16 * (2 * e + c // 4 + 1))
                if not (isinstance(e, int) and e == 0 and c < 2):
                    hold(pool, y_chunk, CH * e + c - 1)
                nc.gpsimd.tensor_copy(w2_hl[:, c % 2, 0], w2_raw[:, c % 4]).then_inc(w2_hi, 1)

            def store(e):
                for i in range(NST):
                    hold(pool, y_ready, NST * e + i + 1)
                    pool.indirect_dma_start(
                        out=out, out_offset=bass.IndirectOffsetOnAxis(ap=tok[:, i:i + 1].bitcast(U32), axis=0),
                        in_=y_sb[:, i, :], in_offset=None, bounds_check=T - 1, oob_is_err=False).then_inc(stored, 16)

            def body(e, first=False):
                split_w2(e, 0)
                split_w2(e, 1)
                if not first:
                    store(e - 1)
                hold(pool, res_in, 16 * (e + 1))
                hold(pool, b2_in, 16 * (e + 1))
                if not first:
                    hold(pool, stored, 16 * NST * e)
                nc.gpsimd.tensor_copy(tok[:], res[:, :, D].bitcast(I32)).then_inc(res_ready, 1)
                nc.gpsimd.tensor_tensor(res_b[:], res[:, :, 0:D], b2_sb[:, 0:1, :].broadcast_to([TP, NST, D]),
                                        ALU.add).then_inc(res_ready, 1)
                for c in range(2, CH):
                    split_w2(e, c)

            body(0, first=True)
            with pool.Fori(1, E) as e:
                body(e)
            store(E - 1)
            hold(pool, stored, 16 * NST * E)

        @block.scalar
        def _(act):
            act.wait_ge(cst_in, 32)
            nc.scalar.activation(b1s[:], b1_sb[:], ACT.Copy, scale=STRETCH).then_inc(b1_scaled, 1)
            act.wait_ge(b1_scaled, 1)

            def split_w1(e, c):
                act.wait_ge(w1_in[c % 4], 16 * (2 * e + c // 4 + 1))
                if not (isinstance(e, int) and e == 0 and c < 2):
                    act.wait_ge(h_out, FT * e + NF * (c - 1))
                nc.scalar.copy(w1_hl[:, c % 2, 0], w1_raw[:, c % 4]).then_inc(w1_hi, 1)

            def split_slots(e):
                for k in range(KC):
                    act.wait_ge(xs_turned, KC * e + k + 1)
                    nc.scalar.copy(xs_hl[:, 0, k, :], ps_h[:, k, 0:CAP]).then_inc(xs_hi, 1)

            def gelu(e, f):
                act.wait_ge(h_out, FT * e + f + 1)
                if not (isinstance(e, int) and e == 0 and f < 2):
                    act.wait_ge(h_lo, FT * e + f - 1)
                nc.scalar.activation(hid[:, f % 2, :], ps_h[:, f % 4, 0:CAP], ACT.Gelu,
                                     bias=b1s[:, e, f:f + 1],
                                     scale=STRETCH).then_inc(gelu_done, 1)

            def body(e, last=False):
                for c in range(CH):
                    if not (last and c == CH - 1):
                        split_w1(e + (c + 1) // CH, (c + 1) % CH)
                    for f in (NF * c, NF * c + 1):
                        gelu(e, f)
                    if c == CH - 1 and not last:
                        split_slots(e + 1)

            split_w1(0, 0)
            split_slots(0)
            body(0)
            with act.Fori(1, E - 1) as e:
                body(e)
            body(E - 1, last=True)

        @block.vector
        def _(dve):
            v = nc.vector

            def less(dst, whole, hi):
                return v.tensor_tensor(dst, whole, hi.bitcast(F32), ALU.subtract)

            def split_w1(e, c):
                dve.wait_ge(w1_hi, CH * e + c + 1)
                less(w1_hl[:, c % 2, 1], w1_raw[:, c % 4], w1_hl[:, c % 2, 0]).then_inc(w1_lo, 1)

            def split_w2(e, c):
                dve.wait_ge(w2_hi, CH * e + c + 1)
                less(w2_hl[:, c % 2, 1], w2_raw[:, c % 4], w2_hl[:, c % 2, 0]).then_inc(w2_lo, 1)

            def split_slots(e):
                for k in range(KC):
                    dve.wait_ge(xs_hi, KC * e + k + 1)
                    less(xs_hl[:, 1, k, :], ps_h[:, k, 0:CAP], xs_hl[:, 0, k, :]).then_inc(xs_lo, 1)

            def split_hidden(e, f):
                dve.wait_ge(gelu_done, FT * e + f + 1)
                if not (isinstance(e, int) and e == 0 and f < 4):
                    dve.wait_ge(y_chunk, CH * e + f // 2 - 1)
                v.tensor_copy(hid_hl[:, f % 4, 0, :], hid[:, f % 2, :]).then_inc(h_hi, 1)
                dve.wait_ge(h_hi, FT * e + f + 1)
                less(hid_hl[:, f % 4, 1, :], hid[:, f % 2, :], hid_hl[:, f % 4, 0, :]).then_inc(h_lo, 1)

            def results(e):
                dve.wait_ge(y_chunk, CH * (e + 1))
                dve.wait_ge(res_ready, 2 * e + 2)
                for i in range(NST):
                    v.scalar_tensor_tensor(out=y_sb[:, i, :], in0=ps_y[0:TP, i, :], scalar=1.0 / STRETCH,
                                           in1=res_b[:, i, :], op0=ALU.mult, op1=ALU.add).then_inc(y_ready, 1)

            def body(e, first=False, last=False):
                for c in range(CH):
                    if not (last and c == CH - 1):
                        split_w1(e + (c + 1) // CH, (c + 1) % CH)
                    split_w2(e, c)
                    for f in (NF * c, NF * c + 1):
                        split_hidden(e, f)
                    if c == 0 and not first:
                        results(e - 1)
                    if c == CH - 1 and not last:
                        split_slots(e + 1)

            split_w1(0, 0)
            split_slots(0)
            body(0, first=True)
            with dve.Fori(1, E - 1) as e:
                body(e)
            body(E - 1, last=True)
            results(E - 1)

        @block.tensor
        def _(pe):
            mm = nc.tensor.matmul

            def turn_slots(e):
                pe.wait_ge(xs_in_s, 16 * (e + 1))
                for k in range(KC):
                    if not (isinstance(e, int) and e == 0):
                        pe.wait_ge(gelu_done, FT * e - KC + k + 1)
                    for i in range(NST):
                        last = nc.tensor.transpose(ps_h[:, k, i * TP:(i + 1) * TP], xs_in[:, i, k * P:(k + 1) * P], idt[:])
                    last.then_inc(xs_turned, 1)

            def hidden(e, c):
                pe.wait_ge(w1_lo, CH * e + c + 1)
                for m in range(NF):
                    f = NF * c + m
                    if c < 2:
                        pe.wait_ge(xs_lo, KC * (e + 1))
                    else:
                        pe.wait_ge(gelu_done, FT * e + f - 3)
                    for k in range(KC):
                        for n, (a, d) in enumerate(three):
                            last = mm(ps_h[:, f % 4, 0:CAP], w1_hl[:, c % 2, a, k, m * P:(m + 1) * P],
                                      xs_hl[:, d, k, :], start=(k == 0 and n == 0), stop=(k == KC - 1 and n == 2))
                    last.then_inc(h_out, 1)

            def outputs(e, c, tiles=range(NF)):
                if 0 in tiles:
                    pe.wait_ge(w2_lo, CH * e + c + 1)
                for m in tiles:
                    f = NF * c + m
                    pe.wait_ge(h_lo, FT * e + f + 1)
                    for i in range(NST):
                        if f == 0 and not (isinstance(e, int) and e == 0):
                            pe.wait_ge(y_ready, NST * (e - 1) + i + 1)
                        for n, (a, d) in enumerate(three):
                            last = mm(ps_y[0:TP, i, :], hid_hl[:, f % 4, a, i * TP:(i + 1) * TP],
                                      w2_hl[:, c % 2, d, m, :], start=(f == 0 and n == 0), stop=(f == FT - 1 and n == 2))
                if NF - 1 in tiles:
                    last.then_inc(y_chunk, 1)

            def body(e, last=False):
                for c in range(CH - 2):
                    hidden(e, c + 1)
                    outputs(e, c)
                hidden(e, CH - 1)
                outputs(e, CH - 2, (0,))
                if not last:
                    turn_slots(e + 1)
                outputs(e, CH - 2, (1,))
                if not last:
                    hidden(e + 1, 0)
                outputs(e, CH - 1)

            pe.wait_ge(cst_in, 32)
            turn_slots(0)
            hidden(0, 0)
            body(0)
            with pe.Fori(1, E - 1) as e:
                body(e)
            body(E - 1, last=True)


def cross_attention_experts(nc, x, ctx_t, wq_t, wk_t, wv_t, wo_t, w_sw, b_sw, w1, b1, w2, b2, consts, out):
    sh = Shapes(x, ctx_t, w1, w2)
    slots = nc.dram_tensor("slots", (sh.T, sh.ROW), F32, kind="Internal").ap()
    out_rows = out.rearrange("b l d -> (b l) d")
    attention_phase(nc, sh, x, ctx_t, wk_t, wv_t, wq_t, wo_t, w_sw, b_sw, consts, slots, out_rows)
    expert_phase(nc, sh, w1, w2, b1, b2, consts, slots, out_rows)


def _constants(tokens_per_tile, experts, capacity):
    import numpy as np

    tp = tokens_per_tile
    c = np.zeros((P, C_END), np.float32)
    c[:, C_ID:C_ID + P] = np.eye(P)
    c[:tp, C_LOW:C_LOW + tp] = np.triu(np.ones((tp, tp)), 1)
    c[:tp, C_ONE:C_ONE + tp] = 1
    c[:, C_BASE:C_BASE + 2 * experts] = np.tile(np.arange(experts) * capacity, 2)
    c[:, C_RANK:C_RANK + 2 * experts] = np.tile(experts - np.arange(experts), 2)
    c[:, C_TOK] = np.arange(P)
    c[:, C_TOK + 1] = np.arange(P) + tp
    return c


def kernel(x, ctx_1024, L0_xattn_Wq, L0_xattn_Wk, L0_xattn_Wv, L0_xattn_Wo, L0_ffn_W_sw, L0_ffn_b_sw,
           L0_ffn_W1, L0_ffn_b1, L0_ffn_W2, L0_ffn_b2):
    import numpy as np
    import concourse.bacc as bacc
    from concourse.bass_utils import run_bass_kernel_spmd

    B, L, D = x.shape
    S = ctx_1024.shape[1]
    E, _, F = L0_ffn_W1.shape
    KC, CH = D // P, F // 256

    def columns(w):
        return np.asarray(w).T.reshape(KC, P, -1).transpose(1, 0, 2)

    arrays = {
        "x": np.asarray(x),
        "ctx_t": np.asarray(ctx_1024).transpose(0, 2, 1).reshape(B, KC, P, S),
        "wq_t": columns(L0_xattn_Wq), "wk_t": columns(L0_xattn_Wk),
        "wv_t": columns(L0_xattn_Wv), "wo_t": columns(L0_xattn_Wo),
        "w_sw": np.asarray(L0_ffn_W_sw).reshape(KC, P, E).transpose(1, 0, 2),
        "b_sw": np.asarray(L0_ffn_b_sw),
        "w1": np.asarray(L0_ffn_W1).reshape(E, KC, P, CH, F // CH).transpose(0, 3, 2, 1, 4),
        "b1": np.asarray(L0_ffn_b1).reshape(E, F // P, P).transpose(2, 0, 1),
        "w2": np.asarray(L0_ffn_W2).reshape(E, CH, F // CH // P, P, D).transpose(0, 1, 3, 2, 4),
        "b2": np.asarray(L0_ffn_b2),
        "consts": _constants(112, E, B * L // E),
    }
    arrays = {n: np.ascontiguousarray(a) for n, a in arrays.items()}
    nc = bacc.Bacc("TRN2", target_bir_lowering=False, num_devices=1)
    ins = {n: nc.dram_tensor(n, a.shape, mybir.dt.from_np(a.dtype), kind="ExternalInput").ap() for n, a in arrays.items()}
    out = nc.dram_tensor("out", (B, L, D), F32, kind="ExternalOutput").ap()
    cross_attention_experts(nc, out=out, **ins)
    r = run_bass_kernel_spmd(nc, [arrays], core_ids=[0])
    return r.results[0]["out"]
```

```python
from contextlib import ExitStack

import concourse.bass as bass
from concourse import mybir

ALU = mybir.AluOpType
ACT = mybir.ActivationFunctionType
AX_X = mybir.AxisListType.X
F32 = mybir.dt.float32
F32R = mybir.dt.float32r
BF16 = mybir.dt.bfloat16
I32 = mybir.dt.int32
U32 = mybir.dt.uint32

P = 128
EPS = 1e-5
STRETCH = 2.0 ** 0.5 / 1.41421
NOWHERE = 65536.0

C_ID, C_LOW, C_ONE, C_BASE, C_RANK, C_TOK, C_END = 0, 128, 240, 352, 368, 384, 386


def wait_alone(eng, sem, count, settled):
    if not isinstance(count, int):
        count = eng.compute_val(count)
        eng.wait_ge(settled, 1)
    eng.wait_ge(sem, count)


def later(eng, sem, count):
    if not (isinstance(count, int) and count <= 0):
        eng.wait_ge(sem, count)


MID_LINKS = 37


class Links:

    def __init__(self, eng, sem):
        self.eng, self.sem, self.base, self.n = eng, sem, 0, 0

    def __call__(self, instruction):
        instruction.then_inc(self.sem, 1)
        self.n += 1

    def count(self):
        return self.base + self.n

    def done(self):
        self.eng.wait_ge(self.sem, self.count())


class Shapes:
    def __init__(self, x, ctx_t, w1, w2):
        self.B, self.L, self.D = x.shape
        self.S = ctx_t.shape[3]
        self.H, self.HD = 16, 32
        self.E, self.CH = w1.shape[0], w1.shape[1]
        self.FC = w1.shape[4]
        self.F = self.CH * self.FC
        self.T = self.B * self.L
        self.CAP = self.T // self.E
        self.TP = 112
        self.NT = self.L // self.TP
        self.KC = self.D // P
        self.SP = 125
        self.NS = self.S // self.SP
        self.G = self.H // 4
        self.HALF = self.S // 2
        self.ROW = 2 * self.D + 4


def attention_phase(nc, sh, x, ctx_t, wk_t, wv_t, wq_t, wo_t, w_sw, b_sw, consts, slots, out):
    B, L, D, S, KC, G, NS, TP, NT = sh.B, sh.L, sh.D, sh.S, sh.KC, sh.G, sh.NS, sh.TP, sh.NT
    SP, HALF, HD, ROW, E, CAP, T = sh.SP, sh.HALF, sh.HD, sh.ROW, sh.E, sh.CAP, sh.T
    NI = G * NS
    SCALE = float(HD) ** -0.5
    KQ = 12 * 16

    with ExitStack() as ctx:
        def sb(name, shape, dt=F32):
            return ctx.enter_context(nc.sbuf_tensor(name, shape, dt))

        def sem(name):
            return ctx.enter_context(nc.semaphore(name))

        ps_s = ctx.enter_context(nc.psum_tensor("ps_scores", [P, 2, 2, 512], F32))
        ps_o = ctx.enter_context(nc.psum_tensor("ps_o", [P, 512], F32))
        ps_a = ctx.enter_context(nc.psum_tensor("ps_a", [P, 512], F32))
        ps_b = ctx.enter_context(nc.psum_tensor("ps_b", [P, 512], F32))
        ps_c = ctx.enter_context(nc.psum_tensor("ps_c", [P, 512], F32))

        w_hl = {n: sb(f"w{n}_hl", [P, 2, KC, D], F32R) for n in "kvqo"}
        sw_raw = sb("sw_raw", [P, KC, E])
        sw_hl = sb("sw_hl", [P, KC, P], F32R)
        cst = sb("cst", [P, C_END])
        low16 = sb("low16", [TP, TP], BF16)
        one16 = sb("one16", [TP, TP], BF16)
        bsw = sb("bsw", [TP, NT, E])
        mhalf = sb("mhalf", [TP, NT])

        raw = sb("ctx_raw", [P, 2, S])
        ctx_hl = sb("ctx_hl", [P, 2, KC, S], F32R)
        v_sb = sb("v_sb", [P, NS, D])
        kq_hl = sb("kq_hl", [P, 2, 2, 4 * L], F32R)
        k_st = sb("k_st", [P, 2, 4, S], F32R)
        q_st = sb("q_st", [P, 4, G, L], F32R)
        probs = sb("probs", [P, 3, 4, L])
        tok_hl = sb("tok_hl", [P, 2, KC, L], F32R)
        o_hl = sb("o_hl", [P, 2, G, L], F32R)
        x_in_all = sb("x_in", [P, NT, D])
        x_in = x_in_all[0:TP]
        x_res_all = sb("x_res", [P, NT, D])
        x_res = x_res_all[0:TP]
        rows_all = sb("rows", [P, NT, ROW])
        rows = rows_all[0:TP]
        xn2 = sb("xn2", [TP, NT, D])
        st1 = sb("st1", [TP, NT, 6])
        st2 = sb("st2", [TP, NT, 6])
        mv1 = sb("mv1", [TP, NT, 2])
        mv2 = sb("mv2", [TP, NT, 2])
        var1 = sb("var1", [TP, NT])
        var2 = sb("var2", [TP, NT])
        rstd1 = sb("rstd1", [TP, NT])
        rstd2 = sb("rstd2", [TP, NT])
        lg0 = sb("lg0", [TP, NT, E])
        lg = sb("lg", [TP, NT, E])
        zed = sb("zed", [TP, NT, E])
        cand = sb("cand", [TP, NT, E])
        hot = sb("hot", [TP, NT, E])
        hot16 = sb("hot16", [TP, NT, E], BF16)
        sgp = sb("sgp", [TP, NT, E])
        sgn = sb("sgn", [TP, NT, E])
        prb = sb("prb", [TP, NT, E])
        posb = sb("posb", [TP, NT, E])
        eoff = sb("eoff", [TP, NT, E])
        cum = sb("cum", [TP, E])
        red = sb("red", [TP, 12, NT])
        slot_i = sb("slot_i", [TP, NT], I32)
        drop_i = sb("drop_i", [TP, NT], I32)

        cst_in = sem("cst_in")
        w_in = [sem(f"w_in{i}") for i in range(4)]
        raw_in = [sem(f"raw_in{k}") for k in range(4)]
        x_in_s = sem("x_in_s")
        xres_in = sem("xres_in")
        kst_in = [sem("kst_in0"), sem("kst_in1")]
        qst_in = sem("qst_in")
        sent = sem("sent")
        k_proj, v_proj, q_proj = sem("k_proj"), sem("v_proj"), sem("q_proj")
        xn_turned, wo_out, x2_turned = sem("xn_turned"), sem("wo_out"), sem("x2_turned")
        logits_out, pos_out = sem("logits_out"), sem("pos_out")
        scores_out, pv_out = sem("scores_out"), sem("pv_out")
        w_hi, w_lo = sem("w_hi"), sem("w_lo")
        ctx_hi, ctx_lo = sem("ctx_hi"), sem("ctx_lo")
        k_hi, k_lo, q_hi, q_lo = sem("k_hi"), sem("k_lo"), sem("q_hi"), sem("q_lo")
        xnt_hi, xnt_lo, o_hi, o_lo = sem("xnt_hi"), sem("xnt_lo"), sem("o_hi"), sem("o_lo")
        x2t_hi, x2t_lo = sem("x2t_hi"), sem("x2t_lo")
        v_ready, probs_ready = sem("v_ready"), sem("probs_ready")
        router_sig = sem("router_sig")
        prep, mhalf_set = sem("prep"), sem("mhalf_set")
        cleared = sem("cleared")
        var1_ready, var2_ready = sem("var1_ready"), sem("var2_ready")
        rstd1_ready, rstd2_ready = sem("rstd1_ready"), sem("rstd2_ready")
        xn_ready, x2_ready, xn2_ready = sem("xn_ready"), sem("x2_ready"), sem("xn2_ready")
        z_ready, hot_ready, rows_ready = sem("z_ready"), sem("hot_ready"), sem("rows_ready")
        dve_link, pool_link = sem("dve_link"), sem("pool_link")

        ident = cst[0:TP, C_ID:C_ID + TP]
        three = ((0, 0), (0, 1), (1, 0))
        w_order = (("k", wk_t), ("v", wv_t), ("q", wq_t), ("o", wo_t))

        def as_weights(t, dims):
            return t.rearrange(f"p {dims} -> p ({dims})")[:, 0:KC * D].rearrange("p (c d) -> p c d", d=D)

        w_tmp = (v_sb[:, 0:4, :], as_weights(probs[:], "a b c"), as_weights(rows_all[:], "a b"),
                 as_weights(probs[:], "a b c"))
        K_BUF, Q_BUF = (0, 0, 1, 0), 1

        def ctx_raw(k):
            return raw[:, k, :] if k < 2 else (x_in_all, x_res_all)[k - 2][:].rearrange("p i d -> p (i d)")[:, 0:S]

        def k_bank(g, h):
            return ((ps_a, ps_b), (ps_b, ps_c), (ps_b, ps_a), (ps_c, ps_a))[g][h]

        def v_bank(t):
            return (ps_b, ps_c, ps_a, ps_a, ps_b, ps_c)[t]

        def turn_bank(b, i):
            return ((ps_a, ps_b) if isinstance(b, int) and b == 0 else (ps_b, ps_c))[i]

        def q_bank(b, i):
            return ((ps_c, ps_a) if isinstance(b, int) and b == 0 else (ps_a, ps_b))[i]

        x2_bank = (ps_a, ps_c)
        o_bank = (ps_c, ps_a)

        def hold(eng, s, count):
            wait_alone(eng, s, count, mhalf_set)

        def after(eng, s, count):
            if not (isinstance(count, int) and count <= 0):
                hold(eng, s, count)

        def x_rows(b):
            return x[b].rearrange("(i p) d -> p i d", p=TP)

        block = ctx.enter_context(nc.Block())

        @block.sync
        def _(sp):
            sp.dma_start(w_tmp[0], wk_t).then_inc(w_in[0], 16)
            for k in range(KC):
                sp.dma_start(ctx_raw(k), ctx_t[0, k]).then_inc(raw_in[k], 16)
            sp.dma_start(w_tmp[1], wv_t).then_inc(w_in[1], 16)
            sp.dma_start(w_tmp[2], wq_t).then_inc(w_in[2], 16)
            sp.dma_start(cst[:], consts).then_inc(cst_in, 16)
            sp.dma_start(sw_raw[:], w_sw).then_inc(cst_in, 16)
            sp.dma_start(bsw[:], b_sw.partition_broadcast(TP)[:, None, :].broadcast_to([TP, NT, E])).then_inc(cst_in, 16)
            hold(sp, ctx_lo, 3)
            sp.dma_start(x_in, x_rows(0)).then_inc(x_in_s, 16)
            hold(sp, w_lo, 2)
            sp.dma_start(w_tmp[3], wo_t).then_inc(w_in[3], 16)

            def stack_k(b, g):
                hold(sp, k_lo, 8 * b + 2 * g + 2)
                after(sp, scores_out, NI * b + NS * (g - 1))
                for j in range(4):
                    for s, part in enumerate((0, 0, 1)):
                        sp.dma_start(k_st[32 * s:32 * s + 32, g % 2, j, :].bitcast(F32),
                                     kq_hl[32 * j:32 * j + 32, K_BUF[g], part, 0:S].bitcast(F32)).then_inc(kst_in[g % 2], 16)

            def stack_q(b):
                hold(sp, q_lo, 2 * b + 2)
                after(sp, scores_out, NI * b)
                for j in range(4):
                    for s, part in enumerate((0, 1, 0)):
                        sp.dma_start(q_st[32 * s:32 * s + 32, j, :, :].rearrange("p g l -> p (g l)").bitcast(F32),
                                     kq_hl[32 * j:32 * j + 32, Q_BUF, part, :].bitcast(F32)).then_inc(qst_in, 16)

            def body(b, last=False, first=False):
                if not first:
                    stack_q(b)
                stack_k(b, 0)
                if not last:
                    for k in (0, 1):
                        hold(sp, ctx_lo, 4 * b + k + 1)
                        sp.dma_start(ctx_raw(k), ctx_t[b + 1, k]).then_inc(raw_in[k], 16)
                    hold(sp, ctx_lo, 4 * b + 3)
                    hold(sp, xn_turned, 2 * b + 2)
                    sp.dma_start(x_in, x_rows(b + 1)).then_inc(x_in_s, 16)
                if first:
                    stack_q(b)
                else:
                    hold(sp, x2_ready, 2 * b)
                if not last:
                    hold(sp, ctx_lo, 4 * b + 4)
                    sp.dma_start(ctx_raw(3), ctx_t[b + 1, 3]).then_inc(raw_in[3], 16)
                stack_k(b, 1)
                stack_k(b, 2)
                if not last:
                    hold(sp, xn_turned, 2 * b + 4)
                    sp.dma_start(ctx_raw(2), ctx_t[b + 1, 2]).then_inc(raw_in[2], 16)
                stack_k(b, 3)
                if not last:
                    hold(sp, ctx_lo, 4 * b + 8)
                sp.dma_start(x_res, x_rows(b)).then_inc(xres_in, 16)

            body(0, first=True)
            with sp.Fori(1, B - 1) as b:
                body(b)
            body(B - 1, last=True)

        @block.gpsimd
        def _(pool):
            link = Links(pool, pool_link)
            nc.gpsimd.memset(mhalf[:], -0.5).then_inc(mhalf_set, 1)

            def split_hi(b):
                for k in range(KC):
                    hold(pool, raw_in[k], 16 * (b + 1))
                    if k == 0:
                        after(pool, k_proj, 8 * b)
                    nc.gpsimd.tensor_copy(ctx_hl[:, 0, k, :], ctx_raw(k)).then_inc(ctx_hi, 1)

            def inverse_std(ready, done, mv, var, rstd, n):
                hold(pool, ready, n + 1)
                link(nc.gpsimd.tensor_scalar(var[:], mv[:, :, 1], EPS, None, ALU.add))
                hold(pool, pool_link, link.count())
                nc.gpsimd.tensor_tensor(rstd[:], var[:], mhalf[:], ALU.pow).then_inc(done, 1)

            def scatter(r):
                hold(pool, rows_ready, r + 1)
                for i in range(NT):
                    nc.gpsimd.indirect_dma_start(
                        out=slots, out_offset=bass.IndirectOffsetOnAxis(ap=slot_i[:, i:i + 1].bitcast(U32), axis=0),
                        in_=rows[:, i, :], in_offset=None, bounds_check=T - 1, oob_is_err=False).then_inc(sent, 16)
                for i in range(NT):
                    nc.gpsimd.indirect_dma_start(
                        out=out, out_offset=bass.IndirectOffsetOnAxis(ap=drop_i[:, i:i + 1].bitcast(U32), axis=0),
                        in_=xn2[:, i, :], in_offset=None, bounds_check=T - 1, oob_is_err=False).then_inc(sent, 16)

            split_hi(0)
            hold(pool, mhalf_set, 1)
            inverse_std(var1_ready, rstd1_ready, mv1, var1, rstd1, 0)
            hold(pool, cleared, 2)
            n = T // TP // 4
            for q in range(4):
                dst = slots[q * n * TP:(q + 1) * n * TP, :].rearrange("(i p) c -> p i c", p=TP)
                pool.dma_start(dst, rows[:, 0:1, :].broadcast_to([TP, n, ROW])).then_inc(sent, 16)

            def body(b, first=False, last=False):
                if not first:
                    inverse_std(var2_ready, rstd2_ready, mv2, var2, rstd2, b - 1)
                if not last:
                    inverse_std(var1_ready, rstd1_ready, mv1, var1, rstd1, b + 1)
                    split_hi(b + 1)
                if not first:
                    scatter(b - 1)

            body(0, first=True)
            assert link.n == 2
            with pool.Fori(1, B - 1) as b:
                link.base, link.n = 2 * b, 0
                body(b)
            link.base, link.n = 2 * (B - 1), 0
            body(B - 1, last=True)
            inverse_std(var2_ready, rstd2_ready, mv2, var2, rstd2, B - 1)
            scatter(B - 1)
            hold(pool, sent, 64 * (B + 1))

        @block.scalar
        def _(act):
            for n, (name, _) in enumerate(w_order):
                act.wait_ge(w_in[n], 16)
                nc.scalar.copy(w_hl[name][:, 0], w_tmp[n]).then_inc(w_hi, 1)

            def k_split(b, g, h):
                if h == 0:
                    if g == 0:
                        later(act, kst_in[1], KQ * 2 * b)
                    elif g == 1:
                        act.wait_ge(kst_in[0], KQ * (2 * b + 1))
                    elif g == 2:
                        act.wait_ge(qst_in, KQ * (b + 1))
                    else:
                        act.wait_ge(kst_in[1], KQ * (2 * b + 1))
                act.wait_ge(k_proj, 8 * b + 2 * g + h + 1)
                bank = k_bank(g, h)
                nc.scalar.copy(kq_hl[:, K_BUF[g], 0, h * HALF:(h + 1) * HALF], bank[:, h:h + HALF]).then_inc(k_hi, 1)

            def turned(b, i, source, done, sem_in):
                act.wait_ge(sem_in, 2 * b + i + 1)
                dst = tok_hl[:, 0, :, i * TP:(i + 1) * TP]
                nc.scalar.copy(dst, source[:, 0:KC * TP].rearrange("p (c t) -> p c t", t=TP)).then_inc(done, 1)

            def values(b, t):
                act.wait_ge(v_proj, NS * b + t + 1)
                nc.scalar.copy(v_sb[0:SP, t, :], v_bank(t)[0:SP, :]).then_inc(v_ready, 1)

            def queries(b, i):
                act.wait_ge(q_proj, 2 * b + i + 1)
                if i == 0 and not (isinstance(b, int) and b == 0):
                    act.wait_ge(kst_in[0], KQ * 2 * b)
                nc.scalar.activation(kq_hl[:, Q_BUF, 0, 2 * L * i:2 * L * (i + 1)], q_bank(b, i)[:, 0:2 * L],
                                     ACT.Copy, scale=SCALE).then_inc(q_hi, 1)

            def sigmoid(b, i):
                act.wait_ge(scores_out, NI * b + i + 1)
                nc.scalar.activation(probs[0:SP, i % 3].rearrange("p (a h) l -> p a (h l)", a=2),
                                     ps_s[0:SP, i % 2, :, 0:2 * L], ACT.Sigmoid).then_inc(probs_ready, 1)

            def attended(b, g):
                act.wait_ge(pv_out, NI * b + NS * (g + 1))
                nc.scalar.copy(o_hl[:, 0, g, :], ps_o[:, 0:L]).then_inc(o_hi, 1)

            def router(r):
                act.wait_ge(z_ready, r + 1)
                nc.scalar.activation(sgp[:], zed[:], ACT.Sigmoid).then_inc(router_sig, 1)
                nc.scalar.activation(sgn[:], zed[:], ACT.Sigmoid, scale=-1.0).then_inc(router_sig, 1)

            def body(b, first=False, last=False):
                k_split(b, 0, 0)
                k_split(b, 0, 1)
                for t in (0, 1, 2):
                    values(b, t)
                k_split(b, 1, 0)
                k_split(b, 1, 1)
                for t in (3, 4, 5):
                    values(b, t)
                if first:
                    for i in range(NT):
                        turned(0, i, turn_bank(0, i), xnt_hi, xn_turned)
                    for i in range(2):
                        queries(0, i)
                    act.wait_ge(w_lo, 4)
                for i in range(NI):
                    sigmoid(b, i)
                    if i in (2, 5, 8, 11):
                        k_split(b, 2 + i // 6, (i // 3) % 2)
                    if i in (7, 13, 19):
                        attended(b, i // 6 - 1)
                    if not first and i in (0, 1):
                        turned(b - 1, i, x2_bank[i], x2t_hi, x2_turned)
                    if not first and i == 9:
                        router(b - 1)
                    if not last and i in (12, 13):
                        turned(b + 1, i - 12, turn_bank(b + 1, i - 12), xnt_hi, xn_turned)
                    if not last and i in (15, 17):
                        queries(b + 1, i // 17)
                attended(b, G - 1)

            body(0, first=True)
            with act.Fori(1, B - 1) as b:
                body(b)
            body(B - 1, last=True)
            turned(B - 1, 0, ps_c, x2t_hi, x2_turned)
            turned(B - 1, 1, ps_b, x2t_hi, x2_turned)
            router(B - 1)

        @block.vector
        def _(dve):
            v = nc.vector
            link = Links(dve, dve_link)

            def less(dst, whole, hi, scale=None):
                if scale is None:
                    return v.tensor_tensor(dst, whole, hi.bitcast(F32), ALU.subtract)
                return v.scalar_tensor_tensor(out=dst, in0=whole, scalar=scale, in1=hi.bitcast(F32),
                                              op0=ALU.mult, op1=ALU.subtract)

            v.memset(cum[:], 0.0).then_inc(prep, 1)

            def split_lo(b, chunks=range(KC)):
                for k in chunks:
                    dve.wait_ge(ctx_hi, 4 * b + k + 1)
                    less(ctx_hl[:, 1, k, :], ctx_raw(k), ctx_hl[:, 0, k, :]).then_inc(ctx_lo, 1)

            def norm_stats(src, st, mv, ready, waits=()):
                for s, c in waits:
                    later(dve, s, c)
                for i in range(NT):
                    link(v.bn_stats(st[:, i, :], src(i)))
                hold(dve, dve_link, link.count())
                for i in range(NT):
                    ins = v.bn_aggr(mv[:, i, :], st[:, i, :])
                    if i < NT - 1:
                        link(ins)
                    else:
                        ins.then_inc(ready, 1)

            def norm1_stats(b):
                norm_stats(lambda i: x_in[:, i, :], st1, mv1, var1_ready, ((x_in_s, 16 * (b + 1)),))

            def norm1(b):
                dve.wait_ge(rstd1_ready, b + 1)
                for i in range(NT):
                    v.tensor_scalar(x_in[:, i, :], x_in[:, i, :], mv1[:, i, 0:1], rstd1[:, i:i + 1],
                                    ALU.subtract, ALU.mult).then_inc(xn_ready, 1)

            def k_split(b, g, h):
                dve.wait_ge(k_hi, 8 * b + 2 * g + h + 1)
                cols = slice(h * HALF, (h + 1) * HALF)
                less(kq_hl[:, K_BUF[g], 1, cols], k_bank(g, h)[:, h:h + HALF],
                     kq_hl[:, K_BUF[g], 0, cols]).then_inc(k_lo, 1)

            def turned(b, i, source, ready, done):
                dve.wait_ge(ready, 2 * b + i + 1)
                cols = slice(i * TP, (i + 1) * TP)
                less(tok_hl[:, 1, :, cols], source[:, 0:KC * TP].rearrange("p (c t) -> p c t", t=TP),
                     tok_hl[:, 0, :, cols]).then_inc(done, 1)

            def queries(b, i):
                dve.wait_ge(q_hi, 2 * b + i + 1)
                cols = slice(2 * L * i, 2 * L * (i + 1))
                less(kq_hl[:, Q_BUF, 1, cols], q_bank(b, i)[:, 0:2 * L], kq_hl[:, Q_BUF, 0, cols], SCALE).then_inc(q_lo, 1)

            def attended(b, g):
                dve.wait_ge(o_hi, G * b + g + 1)
                less(o_hl[:, 1, g, :], ps_o[:, 0:L], o_hl[:, 0, g, :]).then_inc(o_lo, 1)

            def residual(r, i, banks=o_bank):
                if i == 0:
                    dve.wait_ge(sent, 64 * (r + 1))
                    dve.wait_ge(xres_in, 16 * (r + 1))
                dve.wait_ge(wo_out, 2 * r + i + 1)
                v.tensor_tensor(rows[:, i, D:2 * D], banks[i][0:TP, 0:D], x_res[:, i, :],
                                ALU.add).then_inc(x2_ready, 1)

            def norm2_stats(r):
                norm_stats(lambda i: rows[:, i, D:2 * D], st2, mv2, var2_ready, ((x2_ready, 2 * r + 2),))

            def norm2(r):
                dve.wait_ge(rstd2_ready, r + 1)
                for i in range(NT):
                    v.tensor_scalar(xn2[:, i, :], rows[:, i, D:2 * D], mv2[:, i, 0:1], rstd2[:, i:i + 1],
                                    ALU.subtract, ALU.mult).then_inc(xn2_ready, 1)

            def wide(t, n=E):
                return t[:, :, None].broadcast_to([TP, NT, n])

            mx, best, tot, rtot, pmax, rpmax, factor, pos, eslot, kept, place, spare = (red[:, n, :] for n in range(12))
            base = cst[0:TP, C_BASE:C_BASE + NT * E].rearrange("p (i e) -> p i e", e=E)
            rank = cst[0:TP, C_RANK:C_RANK + NT * E].rearrange("p (i e) -> p i e", e=E)
            token = cst[0:TP, C_TOK:C_TOK + NT]

            def choose(r, bank):
                dve.wait_ge(logits_out, r + 1)
                lo = bank[0:TP, 0:NT * P].rearrange("p (i n) -> p i n", n=P)
                link(v.tensor_tensor(lg0[:], lo[:, :, 0:E], bsw[:], ALU.add))
                link.done()
                link(v.tensor_tensor(lg[:], lo[:, :, E:2 * E], lg0[:], ALU.add))
                link.done()
                link(v.tensor_reduce(mx, lg[:], AX_X, ALU.max))
                link.done()
                v.tensor_tensor(zed[:], lg[:], wide(mx), ALU.subtract).then_inc(z_ready, 1)
                link(v.tensor_tensor(cand[:], lg[:], wide(mx), ALU.is_equal))
                link.done()
                link(v.tensor_tensor(cand[:], cand[:], rank, ALU.mult))
                link.done()
                link(v.tensor_reduce(best, cand[:], AX_X, ALU.max))
                link.done()
                v.tensor_tensor(hot16[:], cand[:], wide(best), ALU.is_equal).then_inc(hot_ready, 1)
                link(v.tensor_tensor(hot[:], cand[:], wide(best), ALU.is_equal))

            def scale_tokens(r):
                dve.wait_ge(router_sig, 2 * r + 2)
                link(v.reciprocal(sgn[:], sgn[:]))
                link.done()
                link(v.tensor_tensor(prb[:], sgp[:], sgn[:], ALU.mult))
                link.done()
                link(v.tensor_reduce(tot, prb[:], AX_X, ALU.add))
                link.done()
                link(v.reciprocal(rtot, tot))
                link.done()
                link(v.tensor_tensor(prb[:], prb[:], wide(rtot), ALU.mult))
                link.done()
                link(v.tensor_reduce(pmax, prb[:], AX_X, ALU.max))
                link.done()
                link(v.reciprocal(rpmax, pmax))
                link.done()
                link(v.tensor_tensor(factor, pmax, rpmax, ALU.mult))
                link.done()
                for i in range(NT):
                    link(v.tensor_scalar(rows[:, i, 0:D], xn2[:, i, :], factor[:, i:i + 1], None, ALU.mult))

            def place_tokens(r, bank):
                dve.wait_ge(pos_out, r + 1)
                link.done()
                before = bank[0:TP, 0:NT * E].rearrange("p (i e) -> p i e", e=E)
                link(v.tensor_tensor(posb[:], before, cum[:, None, :].broadcast_to([TP, NT, E]), ALU.add))
                link(v.tensor_tensor(eoff[:], hot[:], base, ALU.mult))
                link.done()
                link(v.tensor_tensor(cum[:], bank[0:TP, NT * E:(NT + 1) * E], cum[:], ALU.add))
                link(v.tensor_tensor(posb[:], posb[:], hot[:], ALU.mult))
                link(v.tensor_reduce(eslot, eoff[:], AX_X, ALU.add))
                link.done()
                link(v.tensor_reduce(pos, posb[:], AX_X, ALU.add))
                link.done()
                link(v.tensor_scalar(spare, pos, float(CAP), NOWHERE, ALU.is_ge, ALU.mult))
                link(v.tensor_scalar(kept, pos, float(CAP), NOWHERE, ALU.is_lt, ALU.mult))
                link(v.tensor_tensor(place, pos, eslot, ALU.add))
                link.done()
                link(v.tensor_tensor(slot_i[:], place, spare, ALU.add))
                link(v.tensor_tensor(drop_i[:], token, kept, ALU.add))
                link(v.tensor_copy(rows[:, :, 2 * D].bitcast(I32), token))
                link(v.tensor_scalar(token, token, float(L), None, ALU.add))
                link(v.tensor_tensor(xn2[:, 0, :], rows[:, 0, 0:D], rows[:, 0, D:2 * D], ALU.add))
                link.done()
                v.tensor_tensor(xn2[:, 1, :], rows[:, 1, 0:D], rows[:, 1, D:2 * D], ALU.add).then_inc(rows_ready, 1)

            split_lo(0)
            dve.wait_ge(w_hi, 1)
            less(w_hl["k"][:, 1], w_tmp[0], w_hl["k"][:, 0]).then_inc(w_lo, 1)
            norm1_stats(0)
            norm1(0)
            for n in (1, 2, 3):
                name = w_order[n][0]
                dve.wait_ge(w_hi, n + 1)
                less(w_hl[name][:, 1], w_tmp[n], w_hl[name][:, 0]).then_inc(w_lo, 1)
                if name == "q":
                    dve.wait_ge(w_lo, 3)
                    v.memset(rows[:, 0, 0:2 * D], 0.0).then_inc(cleared, 1)
                    v.memset(rows[:, 0, 2 * D:ROW].bitcast(I32), int(NOWHERE)).then_inc(cleared, 1)
                    v.memset(rows[:, 1, 2 * D:ROW].bitcast(I32), 0).then_inc(prep, 1)
            dve.wait_ge(cst_in, 48)
            v.memset(sw_hl[:].bitcast(I32), 0).then_inc(prep, 1)
            dve.wait_ge(prep, 3)
            v.tensor_copy(sw_hl[:, :, 0:E], sw_raw[:]).then_inc(prep, 1)
            dve.wait_ge(prep, 4)
            less(sw_hl[:, :, E:2 * E], sw_raw[:], sw_hl[:, :, 0:E]).then_inc(prep, 1)
            v.tensor_copy(low16[:], cst[0:TP, C_LOW:C_LOW + TP]).then_inc(prep, 1)
            v.tensor_copy(one16[:], cst[0:TP, C_ONE:C_ONE + TP]).then_inc(prep, 1)

            def body(b, first=False, last=False):
                k_split(b, 0, 0)
                k_split(b, 0, 1)
                if not first:
                    residual(b - 1, 0)
                    residual(b - 1, 1)
                    norm2_stats(b - 1)
                    if not last:
                        norm1_stats(b + 1)
                    norm2(b - 1)
                    if not last:
                        norm1(b + 1)
                k_split(b, 1, 0)
                k_split(b, 1, 1)
                if first:
                    for i in range(NT):
                        turned(0, i, turn_bank(0, i), xnt_hi, xnt_lo)
                    for i in range(2):
                        queries(0, i)
                    norm1_stats(1)
                    norm1(1)
                else:
                    turned(b - 1, 0, x2_bank[0], x2t_hi, x2t_lo)
                k_split(b, 2, 0)
                if not first:
                    turned(b - 1, 1, x2_bank[1], x2t_hi, x2t_lo)
                k_split(b, 2, 1)
                attended(b, 0)
                if not first:
                    choose(b - 1, ps_b)
                k_split(b, 3, 0)
                if not first:
                    scale_tokens(b - 1)
                k_split(b, 3, 1)
                if not last:
                    turned(b + 1, 0, turn_bank(b + 1, 0), xnt_hi, xnt_lo)
                attended(b, 1)
                if not last:
                    turned(b + 1, 1, turn_bank(b + 1, 1), xnt_hi, xnt_lo)
                    split_lo(b + 1, (0, 1))
                    queries(b + 1, 0)
                    split_lo(b + 1, (2, 3))
                    queries(b + 1, 1)
                attended(b, 2)
                if not first:
                    place_tokens(b - 1, ps_c)
                attended(b, 3)

            body(0, first=True)
            start = link.n
            with dve.Fori(1, B - 1) as b:
                link.base, link.n = start + MID_LINKS * (b - 1), 0
                body(b)
                assert link.n == MID_LINKS, link.n
            link.base, link.n = start + MID_LINKS * (B - 2), 0
            body(B - 1, last=True)
            residual(B - 1, 0, (ps_b, ps_a))
            residual(B - 1, 1, (ps_b, ps_a))
            norm2_stats(B - 1)
            norm2(B - 1)
            turned(B - 1, 0, ps_c, x2t_hi, x2t_lo)
            turned(B - 1, 1, ps_b, x2t_hi, x2t_lo)
            choose(B - 1, ps_a)
            scale_tokens(B - 1)
            place_tokens(B - 1, ps_c)

        @block.tensor
        def _(pe):
            mm = nc.tensor.matmul

            def project_k(b, g, h, part=None):
                bank = k_bank(g, h)
                chunks = range(KC) if part is None else ((0,), (1, 2), (3,))[part]
                for k in chunks:
                    if g == 0 and h == 0:
                        pe.wait_ge(ctx_lo, 4 * b + k + 1)
                    for n, (a, c) in enumerate(three):
                        last = mm(bank[:, 0:HALF + 1], w_hl["k"][:, a, k, g * P:(g + 1) * P],
                                  ctx_hl[:, c, k, h * (HALF - 1):h * (HALF - 1) + HALF + 1],
                                  start=(k == 0 and n == 0), stop=(k == KC - 1 and n == 2))
                if part in (None, 2):
                    last.then_inc(k_proj, 1)

            def project_v(b, t):
                for k in range(KC):
                    for n, (a, c) in enumerate(three):
                        last = mm(v_bank(t)[0:SP, :], ctx_hl[:, a, k, t * SP:(t + 1) * SP], w_hl["v"][:, c, k, :],
                                  start=(k == 0 and n == 0), stop=(k == KC - 1 and n == 2))
                last.then_inc(v_proj, 1)

            def project_q(b, i, parts=(0, 1)):
                for part in parts:
                    g = 2 * i + part
                    for k in range(KC):
                        for n, (a, c) in enumerate(three):
                            last = mm(q_bank(b, i)[:, part * L:(part + 1) * L], w_hl["q"][:, a, k, g * P:(g + 1) * P],
                                      tok_hl[:, c, k, :], start=(k == 0 and n == 0), stop=(k == KC - 1 and n == 2))
                if 1 in parts:
                    last.then_inc(q_proj, 1)

            def project_o(r, i, bank):
                for g in range(G):
                    for n, (a, c) in enumerate(three):
                        last = mm(bank[0:TP, :], o_hl[:, a, g, i * TP:(i + 1) * TP], w_hl["o"][:, c, g, :],
                                  start=(g == 0 and n == 0), stop=(g == G - 1 and n == 2))
                last.then_inc(wo_out, 1)

            def turn(src, i, bank, done):
                for k in range(KC):
                    last = nc.tensor.transpose(bank[:, k * TP:(k + 1) * TP], src[:, i, k * P:(k + 1) * P], ident)
                last.then_inc(done, 1)

            def scores(b, i):
                g, t = divmod(i, NS)
                if t == 0:
                    pe.wait_ge(kst_in[g % 2], KQ * (2 * b + g // 2 + 1))
                if i == 0:
                    pe.wait_ge(qst_in, KQ * (b + 1))
                later(pe, probs_ready, NI * b + i - 1)
                for j in range(4):
                    last = mm(ps_s[0:SP, i % 2, j // 2, (j % 2) * L:(j % 2 + 1) * L],
                              k_st[0:96, g % 2, j, t * SP:(t + 1) * SP], q_st[0:96, j, g, :],
                              start=True, stop=True)
                last.then_inc(scores_out, 1)

            def attend(b, i):
                g, t = divmod(i, NS)
                if i == 0:
                    pe.wait_ge(v_ready, NS * (b + 1))
                if t == 0:
                    later(pe, o_lo, G * b + g)
                pe.wait_ge(probs_ready, NI * b + i + 1)
                for j in range(4):
                    h = 4 * g + j
                    last = mm(ps_o[HD * j:HD * (j + 1), 0:L], v_sb[0:SP, t, HD * h:HD * (h + 1)],
                              probs[0:SP, i % 3, j, :], start=(t == 0), stop=(t == NS - 1))
                last.then_inc(pv_out, 1)

            def route(r, bank):
                pe.wait_ge(x2t_lo, 2 * r + 2)
                for i in range(NT):
                    for k in range(KC):
                        for a in (0, 1):
                            last = mm(bank[0:TP, i * P:(i + 1) * P], tok_hl[:, a, k, i * TP:(i + 1) * TP],
                                      sw_hl[:, k, :], start=(k == 0 and a == 0), stop=(k == KC - 1 and a == 1))
                last.then_inc(logits_out, 1)

            def count(r, bank):
                pe.wait_ge(hot_ready, r + 1)
                mm(bank[0:TP, 0:E], low16[:], hot16[:, 0, :], start=True, stop=True)
                mm(bank[0:TP, E:2 * E], low16[:], hot16[:, 1, :], start=True, stop=False)
                mm(bank[0:TP, E:2 * E], one16[:], hot16[:, 0, :], start=False, stop=True)
                mm(bank[0:TP, 2 * E:3 * E], one16[:], hot16[:, 0, :], start=True, stop=False)
                mm(bank[0:TP, 2 * E:3 * E], one16[:], hot16[:, 1, :], start=False, stop=True).then_inc(pos_out, 1)

            def body(b, first=False, last=False):
                if first:
                    pe.wait_ge(w_lo, 1)
                else:
                    pe.wait_ge(q_lo, 2 * b + 1)
                project_k(b, 0, 0)
                if not first:
                    pe.wait_ge(q_lo, 2 * b + 2)
                project_k(b, 0, 1)
                if not first:
                    pe.wait_ge(o_lo, G * b)
                    project_o(b - 1, 0, o_bank[0])
                    pe.wait_ge(k_lo, 8 * b + 1)
                    project_o(b - 1, 1, o_bank[1])
                else:
                    pe.wait_ge(w_lo, 2)
                pe.wait_ge(k_lo, 8 * b + 2)
                project_v(b, 0)
                if not first:
                    pe.wait_ge(x2_ready, 2 * b - 1)
                project_v(b, 1)
                if not first:
                    pe.wait_ge(x2_ready, 2 * b)
                project_v(b, 2)
                pe.wait_ge(v_ready, NS * b + 1)
                project_k(b, 1, 0)
                pe.wait_ge(v_ready, NS * b + 2)
                project_k(b, 1, 1)
                pe.wait_ge(v_ready, NS * b + 3)
                project_v(b, 3)
                pe.wait_ge(k_lo, 8 * b + 3)
                project_v(b, 4)
                pe.wait_ge(k_lo, 8 * b + 4)
                project_v(b, 5)
                if first:
                    pe.wait_ge(cst_in, 48)
                    for i in range(NT):
                        pe.wait_ge(xn_ready, i + 1)
                        pe.wait_ge(v_ready, 4 + i)
                        turn(x_in, i, turn_bank(0, i), xn_turned)
                    pe.wait_ge(w_lo, 3)
                    pe.wait_ge(v_ready, 6)
                    pe.wait_ge(xnt_lo, 2)
                    project_q(0, 0)
                    project_q(0, 1)
                for i in range(NI):
                    scores(b, i)
                    if not first:
                        if i == 0:
                            pe.wait_ge(v_ready, NS * b + 4)
                            pe.wait_ge(xn2_ready, 2 * b - 1)
                            turn(xn2, 0, x2_bank[0], x2_turned)
                            pe.wait_ge(v_ready, NS * b + 5)
                        if i == 1:
                            pe.wait_ge(v_ready, NS * b + 6)
                            pe.wait_ge(xn2_ready, 2 * b)
                            turn(xn2, 1, x2_bank[1], x2_turned)
                        if i == 3:
                            pe.wait_ge(x2t_lo, 2 * b - 1)
                        if i == 6:
                            pe.wait_ge(k_lo, 8 * b + 5)
                            route(b - 1, ps_b)
                    elif i == 3:
                        pe.wait_ge(q_lo, 2)
                    if i == 9:
                        pe.wait_ge(k_lo, 8 * b + 6)
                    if i < 12:
                        project_k(b, 2 + i // 6, (i // 3) % 2, i % 3)
                    if not last:
                        if i == 12:
                            if first:
                                pe.wait_ge(k_lo, 5)
                            else:
                                pe.wait_ge(hot_ready, b)
                            pe.wait_ge(xn_ready, 2 * b + 3)
                            turn(x_in, 0, turn_bank(b + 1, 0), xn_turned)
                        if i == 13:
                            pe.wait_ge(k_lo, 8 * b + 7)
                            pe.wait_ge(xn_ready, 2 * b + 4)
                            turn(x_in, 1, turn_bank(b + 1, 1), xn_turned)
                        if i == 14:
                            pe.wait_ge(k_lo, 8 * b + 8)
                            pe.wait_ge(xnt_lo, 2 * b + 4)
                        if 14 <= i < 18:
                            project_q(b + 1, (i - 14) // 2, (i % 2,))
                    if not first and i == 18:
                        if last:
                            pe.wait_ge(k_lo, 8 * b + 7)
                        count(b - 1, ps_c)
                    if i >= 2:
                        attend(b, i - 2)
                attend(b, NI - 2)
                attend(b, NI - 1)

            body(0, first=True)
            pe.wait_ge(w_lo, 4)
            pe.wait_ge(prep, 7)
            with pe.Fori(1, B - 1) as b:
                body(b)
            body(B - 1, last=True)
            r = B - 1
            pe.wait_ge(k_lo, 8 * B)
            pe.wait_ge(o_lo, G * B)
            project_o(r, 0, ps_b)
            project_o(r, 1, ps_a)
            pe.wait_ge(xn2_ready, 2 * r + 1)
            turn(xn2, 0, ps_c, x2_turned)
            pe.wait_ge(xn2_ready, 2 * r + 2)
            turn(xn2, 1, ps_b, x2_turned)
            route(r, ps_a)
            count(r, ps_c)


def expert_phase(nc, sh, w1, w2, b1, b2, consts, slots, out):
    D, KC, TP, ROW, E, CAP, T, CH, FC = sh.D, sh.KC, sh.TP, sh.ROW, sh.E, sh.CAP, sh.T, sh.CH, sh.FC
    NST = CAP // TP
    NF = FC // P
    FT = CH * NF

    with ExitStack() as ctx:
        def sb(name, shape, dt=F32):
            return ctx.enter_context(nc.sbuf_tensor(name, shape, dt))

        def sem(name):
            return ctx.enter_context(nc.semaphore(name))

        ps_y = ctx.enter_context(nc.psum_tensor("ps_y", [P, 4, 512], F32))
        ps_h = ctx.enter_context(nc.psum_tensor("ps_h", [P, 4, 512], F32))

        idt = sb("idt", [TP, TP])
        b1_sb = sb("b1_sb", [P, E, FT])
        b1s = sb("b1s", [P, E, FT])
        b2_sb = sb("b2_sb", [TP, 2, D])
        xs_in = sb("xs_in", [TP, NST, D])
        res = sb("res", [TP, NST, D + 4])
        res_b = sb("res_b", [TP, NST, D])
        tok = sb("tok", [TP, NST], I32)
        xs_hl = sb("xs_hl", [P, 2, KC, CAP], F32R)
        w1_raw = sb("w1_raw", [P, 4, KC, FC])
        w2_raw = sb("w2_raw", [P, 4, NF, D])
        w1_hl = sb("w1_hl", [P, 2, 2, KC, FC], F32R)
        w2_hl = sb("w2_hl", [P, 2, 2, NF, D], F32R)
        hid = sb("hid", [P, 2, CAP])
        hid_hl = sb("hid_hl", [P, 4, 2, CAP], F32R)
        y_sb = sb("y_sb", [TP, NST, D])

        cst_in = sem("cst_in2")
        xs_in_s, res_in, b2_in = sem("xs_in_s"), sem("res_in"), sem("b2_in")
        w1_in = [sem(f"w1_in{i}") for i in range(4)]
        w2_in = [sem(f"w2_in{i}") for i in range(4)]
        stored = sem("stored")
        b1_scaled = sem("b1_scaled")
        xs_turned, xs_hi, xs_lo = sem("xs_turned"), sem("xs_hi"), sem("xs_lo")
        w1_hi, w1_lo, w2_hi, w2_lo = sem("w1_hi"), sem("w1_lo"), sem("w2_hi"), sem("w2_lo")
        h_out, gelu_done, h_hi, h_lo = sem("h_out"), sem("gelu_done"), sem("h_hi"), sem("h_lo")
        y_chunk, y_ready = sem("y_chunk"), sem("y_ready")
        res_ready = sem("res_ready")

        three = ((0, 0), (0, 1), (1, 0))

        def hold(eng, s, count):
            wait_alone(eng, s, count, b1_scaled)

        def after(eng, s, count):
            if not (isinstance(count, int) and count <= 0):
                hold(eng, s, count)

        block = ctx.enter_context(nc.Block())

        def slot_rows(e):
            return slots.rearrange("(e i p) c -> e p i c", e=E, p=TP)[e]

        @block.sync
        def _(sp):
            def load_chunk(e, c):
                if not (isinstance(e, int) and e == 0 and c < 4):
                    hold(sp, w1_lo, CH * e + c - 3)
                    hold(sp, w2_lo, CH * e + c - 3)
                sp.dma_start(w1_raw[:, c % 4], w1[e, c]).then_inc(w1_in[c % 4], 16)
                sp.dma_start(w2_raw[:, c % 4], w2[e, c]).then_inc(w2_in[c % 4], 16)

            def load_slots(e):
                after(sp, xs_turned, KC * e)
                sp.dma_start(xs_in[:], slot_rows(e)[:, :, 0:D]).then_inc(xs_in_s, 16)

            def load_residual(e):
                after(sp, res_ready, 2 * e)
                sp.dma_start(res[:], slot_rows(e)[:, :, D:ROW]).then_inc(res_in, 16)
                sp.dma_start(b2_sb[:, 0, :], b2[e].partition_broadcast(TP)).then_inc(b2_in, 16)

            load_slots(0)
            sp.dma_start(idt[:], consts[0:TP, C_ID:C_ID + TP]).then_inc(cst_in, 16)
            sp.dma_start(b1_sb[:], b1).then_inc(cst_in, 16)
            for c in range(4):
                load_chunk(0, c)
            load_residual(0)

            def body(e, last=False):
                for c in range(4, CH):
                    load_chunk(e, c)
                    if c == 5 and not last:
                        load_slots(e + 1)
                if not last:
                    for c in range(4):
                        load_chunk(e + 1, c)
                    load_residual(e + 1)

            with sp.Fori(0, E - 1) as e:
                body(e)
            body(E - 1, last=True)

        @block.gpsimd
        def _(pool):
            def split_w2(e, c):
                hold(pool, w2_in[c % 4], 16 * (2 * e + c // 4 + 1))
                if not (isinstance(e, int) and e == 0 and c < 2):
                    hold(pool, y_chunk, CH * e + c - 1)
                nc.gpsimd.tensor_copy(w2_hl[:, c % 2, 0], w2_raw[:, c % 4]).then_inc(w2_hi, 1)

            def store(e):
                for i in range(NST):
                    hold(pool, y_ready, NST * e + i + 1)
                    pool.indirect_dma_start(
                        out=out, out_offset=bass.IndirectOffsetOnAxis(ap=tok[:, i:i + 1].bitcast(U32), axis=0),
                        in_=y_sb[:, i, :], in_offset=None, bounds_check=T - 1, oob_is_err=False).then_inc(stored, 16)

            def body(e, first=False):
                split_w2(e, 0)
                split_w2(e, 1)
                if not first:
                    store(e - 1)
                hold(pool, res_in, 16 * (e + 1))
                hold(pool, b2_in, 16 * (e + 1))
                if not first:
                    hold(pool, stored, 16 * NST * e)
                nc.gpsimd.tensor_copy(tok[:], res[:, :, D].bitcast(I32)).then_inc(res_ready, 1)
                nc.gpsimd.tensor_tensor(res_b[:], res[:, :, 0:D], b2_sb[:, 0:1, :].broadcast_to([TP, NST, D]),
                                        ALU.add).then_inc(res_ready, 1)
                for c in range(2, CH):
                    split_w2(e, c)

            body(0, first=True)
            with pool.Fori(1, E) as e:
                body(e)
            store(E - 1)
            hold(pool, stored, 16 * NST * E)

        @block.scalar
        def _(act):
            act.wait_ge(cst_in, 32)
            nc.scalar.activation(b1s[:], b1_sb[:], ACT.Copy, scale=STRETCH).then_inc(b1_scaled, 1)
            act.wait_ge(b1_scaled, 1)

            def split_w1(e, c):
                act.wait_ge(w1_in[c % 4], 16 * (2 * e + c // 4 + 1))
                if not (isinstance(e, int) and e == 0 and c < 2):
                    act.wait_ge(h_out, FT * e + NF * (c - 1))
                nc.scalar.copy(w1_hl[:, c % 2, 0], w1_raw[:, c % 4]).then_inc(w1_hi, 1)

            def split_slots(e):
                for k in range(KC):
                    act.wait_ge(xs_turned, KC * e + k + 1)
                    nc.scalar.copy(xs_hl[:, 0, k, :], ps_h[:, k, 0:CAP]).then_inc(xs_hi, 1)

            def gelu(e, f):
                act.wait_ge(h_out, FT * e + f + 1)
                if not (isinstance(e, int) and e == 0 and f < 2):
                    act.wait_ge(h_lo, FT * e + f - 1)
                nc.scalar.activation(hid[:, f % 2, :], ps_h[:, f % 4, 0:CAP], ACT.Gelu,
                                     bias=b1s[:, e, f:f + 1],
                                     scale=STRETCH).then_inc(gelu_done, 1)

            def body(e, last=False):
                for c in range(CH):
                    if not (last and c == CH - 1):
                        split_w1(e + (c + 1) // CH, (c + 1) % CH)
                    for f in (NF * c, NF * c + 1):
                        gelu(e, f)
                    if c == CH - 1 and not last:
                        split_slots(e + 1)

            split_w1(0, 0)
            split_slots(0)
            body(0)
            with act.Fori(1, E - 1) as e:
                body(e)
            body(E - 1, last=True)

        @block.vector
        def _(dve):
            v = nc.vector

            def less(dst, whole, hi):
                return v.tensor_tensor(dst, whole, hi.bitcast(F32), ALU.subtract)

            def split_w1(e, c):
                dve.wait_ge(w1_hi, CH * e + c + 1)
                less(w1_hl[:, c % 2, 1], w1_raw[:, c % 4], w1_hl[:, c % 2, 0]).then_inc(w1_lo, 1)

            def split_w2(e, c):
                dve.wait_ge(w2_hi, CH * e + c + 1)
                less(w2_hl[:, c % 2, 1], w2_raw[:, c % 4], w2_hl[:, c % 2, 0]).then_inc(w2_lo, 1)

            def split_slots(e):
                for k in range(KC):
                    dve.wait_ge(xs_hi, KC * e + k + 1)
                    less(xs_hl[:, 1, k, :], ps_h[:, k, 0:CAP], xs_hl[:, 0, k, :]).then_inc(xs_lo, 1)

            def split_hidden(e, f):
                dve.wait_ge(gelu_done, FT * e + f + 1)
                if not (isinstance(e, int) and e == 0 and f < 4):
                    dve.wait_ge(y_chunk, CH * e + f // 2 - 1)
                v.tensor_copy(hid_hl[:, f % 4, 0, :], hid[:, f % 2, :]).then_inc(h_hi, 1)
                dve.wait_ge(h_hi, FT * e + f + 1)
                less(hid_hl[:, f % 4, 1, :], hid[:, f % 2, :], hid_hl[:, f % 4, 0, :]).then_inc(h_lo, 1)

            def results(e):
                dve.wait_ge(y_chunk, CH * (e + 1))
                dve.wait_ge(res_ready, 2 * e + 2)
                for i in range(NST):
                    v.scalar_tensor_tensor(out=y_sb[:, i, :], in0=ps_y[0:TP, i, :], scalar=1.0 / STRETCH,
                                           in1=res_b[:, i, :], op0=ALU.mult, op1=ALU.add).then_inc(y_ready, 1)

            def body(e, first=False, last=False):
                for c in range(CH):
                    if not (last and c == CH - 1):
                        split_w1(e + (c + 1) // CH, (c + 1) % CH)
                    split_w2(e, c)
                    for f in (NF * c, NF * c + 1):
                        split_hidden(e, f)
                    if c == 0 and not first:
                        results(e - 1)
                    if c == CH - 1 and not last:
                        split_slots(e + 1)

            split_w1(0, 0)
            split_slots(0)
            body(0, first=True)
            with dve.Fori(1, E - 1) as e:
                body(e)
            body(E - 1, last=True)
            results(E - 1)

        @block.tensor
        def _(pe):
            mm = nc.tensor.matmul

            def turn_slots(e):
                pe.wait_ge(xs_in_s, 16 * (e + 1))
                for k in range(KC):
                    if not (isinstance(e, int) and e == 0):
                        pe.wait_ge(gelu_done, FT * e - KC + k + 1)
                    for i in range(NST):
                        last = nc.tensor.transpose(ps_h[:, k, i * TP:(i + 1) * TP], xs_in[:, i, k * P:(k + 1) * P], idt[:])
                    last.then_inc(xs_turned, 1)

            def hidden(e, c):
                pe.wait_ge(w1_lo, CH * e + c + 1)
                for m in range(NF):
                    f = NF * c + m
                    if c < 2:
                        pe.wait_ge(xs_lo, KC * (e + 1))
                    else:
                        pe.wait_ge(gelu_done, FT * e + f - 3)
                    for k in range(KC):
                        for n, (a, d) in enumerate(three):
                            last = mm(ps_h[:, f % 4, 0:CAP], w1_hl[:, c % 2, a, k, m * P:(m + 1) * P],
                                      xs_hl[:, d, k, :], start=(k == 0 and n == 0), stop=(k == KC - 1 and n == 2))
                    last.then_inc(h_out, 1)

            def outputs(e, c, tiles=range(NF)):
                if 0 in tiles:
                    pe.wait_ge(w2_lo, CH * e + c + 1)
                for m in tiles:
                    f = NF * c + m
                    pe.wait_ge(h_lo, FT * e + f + 1)
                    for i in range(NST):
                        if f == 0 and not (isinstance(e, int) and e == 0):
                            pe.wait_ge(y_ready, NST * (e - 1) + i + 1)
                        for n, (a, d) in enumerate(three):
                            last = mm(ps_y[0:TP, i, :], hid_hl[:, f % 4, a, i * TP:(i + 1) * TP],
                                      w2_hl[:, c % 2, d, m, :], start=(f == 0 and n == 0), stop=(f == FT - 1 and n == 2))
                if NF - 1 in tiles:
                    last.then_inc(y_chunk, 1)

            def body(e, last=False):
                for c in range(CH - 2):
                    hidden(e, c + 1)
                    outputs(e, c)
                hidden(e, CH - 1)
                outputs(e, CH - 2, (0,))
                if not last:
                    turn_slots(e + 1)
                outputs(e, CH - 2, (1,))
                if not last:
                    hidden(e + 1, 0)
                outputs(e, CH - 1)

            pe.wait_ge(cst_in, 32)
            turn_slots(0)
            hidden(0, 0)
            body(0)
            with pe.Fori(1, E - 1) as e:
                body(e)
            body(E - 1, last=True)


def cross_attention_experts(nc, x, ctx_t, wq_t, wk_t, wv_t, wo_t, w_sw, b_sw, w1, b1, w2, b2, consts, out):
    sh = Shapes(x, ctx_t, w1, w2)
    slots = nc.dram_tensor("slots", (sh.T, sh.ROW), F32, kind="Internal").ap()
    out_rows = out.rearrange("b l d -> (b l) d")
    attention_phase(nc, sh, x, ctx_t, wk_t, wv_t, wq_t, wo_t, w_sw, b_sw, consts, slots, out_rows)
    expert_phase(nc, sh, w1, w2, b1, b2, consts, slots, out_rows)


def _constants(tokens_per_tile, experts, capacity):
    import numpy as np

    tp = tokens_per_tile
    c = np.zeros((P, C_END), np.float32)
    c[:, C_ID:C_ID + P] = np.eye(P)
    c[:tp, C_LOW:C_LOW + tp] = np.triu(np.ones((tp, tp)), 1)
    c[:tp, C_ONE:C_ONE + tp] = 1
    c[:, C_BASE:C_BASE + 2 * experts] = np.tile(np.arange(experts) * capacity, 2)
    c[:, C_RANK:C_RANK + 2 * experts] = np.tile(experts - np.arange(experts), 2)
    c[:, C_TOK] = np.arange(P)
    c[:, C_TOK + 1] = np.arange(P) + tp
    return c


def kernel(x, ctx_1024, L0_xattn_Wq, L0_xattn_Wk, L0_xattn_Wv, L0_xattn_Wo, L0_ffn_W_sw, L0_ffn_b_sw,
           L0_ffn_W1, L0_ffn_b1, L0_ffn_W2, L0_ffn_b2):
    import numpy as np
    import concourse.bacc as bacc
    from concourse.bass_utils import run_bass_kernel_spmd

    B, L, D = x.shape
    S = ctx_1024.shape[1]
    E, _, F = L0_ffn_W1.shape
    KC, CH = D // P, F // 256

    def columns(w):
        return np.asarray(w).T.reshape(KC, P, -1).transpose(1, 0, 2)

    arrays = {
        "x": np.asarray(x),
        "ctx_t": np.asarray(ctx_1024).transpose(0, 2, 1).reshape(B, KC, P, S),
        "wq_t": columns(L0_xattn_Wq), "wk_t": columns(L0_xattn_Wk),
        "wv_t": columns(L0_xattn_Wv), "wo_t": columns(L0_xattn_Wo),
        "w_sw": np.asarray(L0_ffn_W_sw).reshape(KC, P, E).transpose(1, 0, 2),
        "b_sw": np.asarray(L0_ffn_b_sw),
        "w1": np.asarray(L0_ffn_W1).reshape(E, KC, P, CH, F // CH).transpose(0, 3, 2, 1, 4),
        "b1": np.asarray(L0_ffn_b1).reshape(E, F // P, P).transpose(2, 0, 1),
        "w2": np.asarray(L0_ffn_W2).reshape(E, CH, F // CH // P, P, D).transpose(0, 1, 3, 2, 4),
        "b2": np.asarray(L0_ffn_b2),
        "consts": _constants(112, E, B * L // E),
    }
    arrays = {n: np.ascontiguousarray(a) for n, a in arrays.items()}
    nc = bacc.Bacc("TRN2", target_bir_lowering=False, num_devices=1)
    ins = {n: nc.dram_tensor(n, a.shape, mybir.dt.from_np(a.dtype), kind="ExternalInput").ap() for n, a in arrays.items()}
    out = nc.dram_tensor("out", (B, L, D), F32, kind="ExternalOutput").ap()
    cross_attention_experts(nc, out=out, **ins)
    r = run_bass_kernel_spmd(nc, [arrays], core_ids=[0])
    return r.results[0]["out"]
```

```python
from contextlib import ExitStack

import concourse.bass as bass
from concourse import mybir

ALU = mybir.AluOpType
ACT = mybir.ActivationFunctionType
AX_X = mybir.AxisListType.X
F32 = mybir.dt.float32
F32R = mybir.dt.float32r
BF16 = mybir.dt.bfloat16
I32 = mybir.dt.int32
U32 = mybir.dt.uint32

P = 128
EPS = 1e-5
STRETCH = 2.0 ** 0.5 / 1.41421
NOWHERE = 65536.0

C_ID, C_LOW, C_ONE, C_BASE, C_RANK, C_TOK, C_END = 0, 128, 240, 352, 368, 384, 386


def wait_alone(eng, sem, count, settled):
    if not isinstance(count, int):
        count = eng.compute_val(count)
        eng.wait_ge(settled, 1)
    eng.wait_ge(sem, count)


def later(eng, sem, count):
    if not (isinstance(count, int) and count <= 0):
        eng.wait_ge(sem, count)


MID_LINKS = 36


class Links:

    def __init__(self, eng, sem):
        self.eng, self.sem, self.base, self.n = eng, sem, 0, 0

    def __call__(self, instruction):
        instruction.then_inc(self.sem, 1)
        self.n += 1

    def count(self):
        return self.base + self.n

    def done(self):
        self.eng.wait_ge(self.sem, self.count())


class Shapes:
    def __init__(self, x, ctx_t, w1, w2):
        self.B, self.L, self.D = x.shape
        self.S = ctx_t.shape[3]
        self.H, self.HD = 16, 32
        self.E, self.CH = w1.shape[0], w1.shape[1]
        self.FC = w1.shape[4]
        self.F = self.CH * self.FC
        self.T = self.B * self.L
        self.CAP = self.T // self.E
        self.TP = 112
        self.NT = self.L // self.TP
        self.KC = self.D // P
        self.SP = 125
        self.NS = self.S // self.SP
        self.G = self.H // 4
        self.HALF = self.S // 2
        self.ROW = 2 * self.D + 4


def attention_phase(nc, sh, x, ctx_t, wk_t, wv_t, wq_t, wo_t, w_sw, b_sw, consts, slots, loads, out):
    B, L, D, S, KC, G, NS, TP, NT = sh.B, sh.L, sh.D, sh.S, sh.KC, sh.G, sh.NS, sh.TP, sh.NT
    SP, HALF, HD, ROW, E, CAP, T = sh.SP, sh.HALF, sh.HD, sh.ROW, sh.E, sh.CAP, sh.T
    NI = G * NS
    SCALE = float(HD) ** -0.5
    KQ = 12 * 16
    CLEARS = 8

    with ExitStack() as ctx:
        def sb(name, shape, dt=F32):
            return ctx.enter_context(nc.sbuf_tensor(name, shape, dt))

        def sem(name):
            return ctx.enter_context(nc.semaphore(name))

        ps_s = ctx.enter_context(nc.psum_tensor("ps_scores", [P, 2, 2, 512], F32))
        ps_o = ctx.enter_context(nc.psum_tensor("ps_o", [P, 512], F32))
        ps_a = ctx.enter_context(nc.psum_tensor("ps_a", [P, 512], F32))
        ps_b = ctx.enter_context(nc.psum_tensor("ps_b", [P, 512], F32))
        ps_c = ctx.enter_context(nc.psum_tensor("ps_c", [P, 512], F32))

        w_hl = {n: sb(f"w{n}_hl", [P, 2, KC, D], F32R) for n in "kvqo"}
        sw_raw = sb("sw_raw", [P, KC, E])
        sw_hl = sb("sw_hl", [P, KC, P], F32R)
        cst = sb("cst", [P, C_END])
        low16 = sb("low16", [TP, TP], BF16)
        one16 = sb("one16", [TP, TP], BF16)
        bsw = sb("bsw", [TP, NT, E])
        mhalf = sb("mhalf", [TP, NT])

        raw = sb("ctx_raw", [P, 2, S])
        ctx_hl = sb("ctx_hl", [P, 2, KC, S], F32R)
        v_sb = sb("v_sb", [P, NS, D])
        kq_hl = sb("kq_hl", [P, 2, 2, 4 * L], F32R)
        k_st = sb("k_st", [P, 2, 4, S], F32R)
        q_st = sb("q_st", [P, 4, G, L], F32R)
        probs = sb("probs", [P, 3, 4, L])
        tok_hl = sb("tok_hl", [P, 2, KC, L], F32R)
        o_hl = sb("o_hl", [P, 2, G, L], F32R)
        x_in_all = sb("x_in", [P, NT, D])
        x_in = x_in_all[0:TP]
        x_res_all = sb("x_res", [P, NT, D])
        x_res = x_res_all[0:TP]
        rows_all = sb("rows", [P, NT, ROW])
        rows = rows_all[0:TP]
        xn2 = sb("xn2", [TP, NT, D])
        st1 = sb("st1", [TP, NT, 6])
        st2 = sb("st2", [TP, NT, 6])
        mv1 = sb("mv1", [TP, NT, 2])
        mv2 = sb("mv2", [TP, NT, 2])
        var1 = sb("var1", [TP, NT])
        var2 = sb("var2", [TP, NT])
        rstd1 = sb("rstd1", [TP, NT])
        rstd2 = sb("rstd2", [TP, NT])
        lg0 = sb("lg0", [TP, NT, E])
        lg = sb("lg", [TP, NT, E])
        zed = sb("zed", [TP, NT, E])
        cand = sb("cand", [TP, NT, E])
        hot = sb("hot", [TP, NT, E])
        hot16 = sb("hot16", [TP, NT, E], BF16)
        sgp = sb("sgp", [TP, NT, E])
        sgn = sb("sgn", [TP, NT, E])
        prb = sb("prb", [TP, NT, E])
        posb = sb("posb", [TP, NT, E])
        eoff = sb("eoff", [TP, NT, E])
        cum = sb("cum", [TP, E])
        red = sb("red", [TP, 12, NT])
        slot_i = sb("slot_i", [TP, NT], I32)
        drop_i = sb("drop_i", [TP, NT], I32)

        cst_in, router_in = sem("cst_in"), sem("router_in")
        w_in = [sem(f"w_in{i}") for i in range(4)]
        raw_in = [sem(f"raw_in{k}") for k in range(4)]
        x_in_s = sem("x_in_s")
        xres_in = sem("xres_in")
        kst_in = [sem("kst_in0"), sem("kst_in1")]
        qst_in = sem("qst_in")
        sent = sem("sent")
        k_proj, v_proj, q_proj = sem("k_proj"), sem("v_proj"), sem("q_proj")
        xn_turned, wo_out, x2_turned = sem("xn_turned"), sem("wo_out"), sem("x2_turned")
        logits_out, pos_out = sem("logits_out"), sem("pos_out")
        scores_out, pv_out = sem("scores_out"), sem("pv_out")
        w_hi, w_lo = sem("w_hi"), sem("w_lo")
        ctx_hi, ctx_lo, first_hi = sem("ctx_hi"), sem("ctx_lo"), sem("first_hi")
        k_hi, k_lo, q_hi, q_lo = sem("k_hi"), sem("k_lo"), sem("q_hi"), sem("q_lo")
        xnt_hi, xnt_lo, o_hi, o_lo = sem("xnt_hi"), sem("xnt_lo"), sem("o_hi"), sem("o_lo")
        x2t_hi, x2t_lo = sem("x2t_hi"), sem("x2t_lo")
        v_ready, probs_ready = sem("v_ready"), sem("probs_ready")
        router_sig = sem("router_sig")
        prep, mhalf_set = sem("prep"), sem("mhalf_set")
        loads_ready = sem("loads_ready")
        counts_read = sem("counts_read")
        cleared = sem("cleared")
        var1_ready, var2_ready = sem("var1_ready"), sem("var2_ready")
        rstd1_ready, rstd2_ready = sem("rstd1_ready"), sem("rstd2_ready")
        xn_ready, x2_ready, xn2_ready = sem("xn_ready"), sem("x2_ready"), sem("xn2_ready")
        z_ready, hot_ready, rows_ready = sem("z_ready"), sem("hot_ready"), sem("rows_ready")
        dve_link, pool_link = sem("dve_link"), sem("pool_link")

        ident = cst[0:TP, C_ID:C_ID + TP]
        three = ((0, 0), (0, 1), (1, 0))
        w_order = (("k", wk_t), ("v", wv_t), ("q", wq_t), ("o", wo_t))

        def as_weights(t, dims):
            return t.rearrange(f"p {dims} -> p ({dims})")[:, 0:KC * D].rearrange("p (c d) -> p c d", d=D)

        w_tmp = (v_sb[:, 0:4, :], as_weights(probs[:], "a b c"), as_weights(rows_all[:], "a b"),
                 as_weights(probs[:], "a b c"))
        K_BUF, Q_BUF = (0, 0, 1, 0), 1

        def ctx_raw(k):
            return raw[:, k, :] if k < 2 else (x_in_all, x_res_all)[k - 2][:].rearrange("p i d -> p (i d)")[:, 0:S]

        def k_bank(g, h):
            return ((ps_a, ps_b), (ps_b, ps_c), (ps_b, ps_a), (ps_c, ps_a))[g][h]

        def o_out(g):
            return ps_o if g < G - 1 else ps_c

        def v_bank(t):
            return (ps_b, ps_c, ps_a, ps_a, ps_b, ps_c)[t]

        turn_bank, q_bank = (ps_b, ps_c), (ps_a, ps_b)
        x2_bank = (ps_a, ps_c)
        o_bank = (ps_c, ps_a)

        def hold(eng, s, count):
            wait_alone(eng, s, count, mhalf_set)

        def after(eng, s, count):
            if not (isinstance(count, int) and count <= 0):
                hold(eng, s, count)

        def x_rows(b):
            return x[b].rearrange("(i p) d -> p i d", p=TP)

        block = ctx.enter_context(nc.Block())

        @block.sync
        def _(sp):
            sp.dma_start(w_tmp[0], wk_t).then_inc(w_in[0], 16)
            for k in range(KC):
                sp.dma_start(ctx_raw(k), ctx_t[0, k]).then_inc(raw_in[k], 16)
            sp.dma_start(w_tmp[1], wv_t).then_inc(w_in[1], 16)
            sp.dma_start(cst[:], consts).then_inc(cst_in, 16)
            sp.dma_start(w_tmp[2], wq_t).then_inc(w_in[2], 16)
            hold(sp, ctx_lo, 3)
            sp.dma_start(x_in, x_rows(0)).then_inc(x_in_s, 16)
            hold(sp, w_lo, 2)
            sp.dma_start(w_tmp[3], wo_t).then_inc(w_in[3], 16)
            sp.dma_start(sw_raw[:], w_sw).then_inc(router_in, 16)
            sp.dma_start(bsw[:], b_sw.partition_broadcast(TP)[:, None, :].broadcast_to([TP, NT, E])).then_inc(router_in, 16)

            def stack_k(b, g, heads=range(4)):
                if 0 in heads:
                    hold(sp, k_lo, 8 * b + 2 * g + 2)
                    after(sp, scores_out, NI * b + NS * (g - 1))
                for j in heads:
                    for s, part in enumerate((0, 0, 1)):
                        sp.dma_start(k_st[32 * s:32 * s + 32, g % 2, j, :].bitcast(F32),
                                     kq_hl[32 * j:32 * j + 32, K_BUF[g], part, 0:S].bitcast(F32)).then_inc(kst_in[g % 2], 16)

            def stack_q(b):
                hold(sp, q_lo, 2 * b + 2)
                after(sp, scores_out, NI * b)
                for j in range(4):
                    for s, part in enumerate((0, 1, 0)):
                        sp.dma_start(q_st[32 * s:32 * s + 32, j, :, :].rearrange("p g l -> p (g l)").bitcast(F32),
                                     kq_hl[32 * j:32 * j + 32, Q_BUF, part, :].bitcast(F32)).then_inc(qst_in, 16)

            def body(b, last=False, first=False):
                if first:
                    stack_k(b, 0)
                    stack_q(b)
                else:
                    stack_q(b)
                    stack_k(b, 0)
                if not last:
                    hold(sp, ctx_lo, 4 * b + 3)
                    hold(sp, xn_turned, 2 * b + 2)
                    sp.dma_start(x_in, x_rows(b + 1)).then_inc(x_in_s, 16)
                    for k in (0, 1):
                        hold(sp, ctx_lo, 4 * b + k + 1)
                        sp.dma_start(ctx_raw(k), ctx_t[b + 1, k]).then_inc(raw_in[k], 16)
                if not first:
                    hold(sp, x2_ready, 2 * b)
                if not last:
                    hold(sp, ctx_lo, 4 * b + 4)
                    sp.dma_start(ctx_raw(3), ctx_t[b + 1, 3]).then_inc(raw_in[3], 16)
                stack_k(b, 1)
                stack_k(b, 2)
                stack_k(b, 3, (0, 1))
                if not last:
                    hold(sp, xn_turned, 2 * b + 4)
                    sp.dma_start(ctx_raw(2), ctx_t[b + 1, 2]).then_inc(raw_in[2], 16)
                stack_k(b, 3, (2, 3))
                if not last:
                    hold(sp, ctx_lo, 4 * b + 8)
                sp.dma_start(x_res, x_rows(b)).then_inc(xres_in, 16)

            body(0, first=True)
            with sp.Fori(1, B - 1) as b:
                body(b)
            body(B - 1, last=True)

        @block.gpsimd
        def _(pool):
            link = Links(pool, pool_link)
            nc.gpsimd.memset(mhalf[:], -0.5).then_inc(mhalf_set, 1)

            def split_hi(b):
                first = isinstance(b, int) and b == 0
                for k in range(2 if first else 0, KC):
                    hold(pool, raw_in[k], 16 * (b + 1))
                    if k == 0:
                        after(pool, k_proj, 8 * b)
                    nc.gpsimd.tensor_copy(ctx_hl[:, 0, k, :], ctx_raw(k)).then_inc(ctx_hi, 2 if first else 1)

            def inverse_std(ready, done, mv, var, rstd, n):
                hold(pool, ready, n + 1)
                link(nc.gpsimd.tensor_scalar(var[:], mv[:, :, 1], EPS, None, ALU.add))
                hold(pool, pool_link, link.count())
                nc.gpsimd.tensor_tensor(rstd[:], var[:], mhalf[:], ALU.pow).then_inc(done, 1)

            def scatter(r):
                hold(pool, rows_ready, r + 1)
                hold(pool, sent, 64 * r + 16 * CLEARS)
                for i in range(NT):
                    nc.gpsimd.indirect_dma_start(
                        out=slots, out_offset=bass.IndirectOffsetOnAxis(ap=slot_i[:, i:i + 1].bitcast(U32), axis=0),
                        in_=rows[:, i, :], in_offset=None, bounds_check=T - 1, oob_is_err=False).then_inc(sent, 16)
                for i in range(NT):
                    nc.gpsimd.indirect_dma_start(
                        out=out, out_offset=bass.IndirectOffsetOnAxis(ap=drop_i[:, i:i + 1].bitcast(U32), axis=0),
                        in_=xn2[:, i, :], in_offset=None, bounds_check=T - 1, oob_is_err=False).then_inc(sent, 16)

            def clear(parts):
                hold(pool, cleared, 2)
                n = T // TP // CLEARS
                for q in parts:
                    dst = slots[q * n * TP:(q + 1) * n * TP, :].rearrange("(i p) c -> p i c", p=TP)
                    pool.dma_start(dst, rows[:, 0:1, :].broadcast_to([TP, n, ROW])).then_inc(sent, 16)

            split_hi(0)
            hold(pool, mhalf_set, 1)
            inverse_std(var1_ready, rstd1_ready, mv1, var1, rstd1, 0)

            def body(b, first=False, last=False):
                if not first:
                    inverse_std(var2_ready, rstd2_ready, mv2, var2, rstd2, b - 1)
                if first:
                    hold(pool, kst_in[0], KQ)
                    clear(range(3))
                if not last:
                    inverse_std(var1_ready, rstd1_ready, mv1, var1, rstd1, b + 1)
                if first:
                    hold(pool, kst_in[1], KQ)
                    clear(range(3, 5))
                if not last:
                    split_hi(b + 1)
                if first:
                    clear(range(5, CLEARS))
                if not first:
                    scatter(b - 1)

            body(0, first=True)
            assert link.n == 2
            with pool.Fori(1, B - 1) as b:
                link.base, link.n = 2 * b, 0
                body(b)
            link.base, link.n = 2 * (B - 1), 0
            body(B - 1, last=True)
            inverse_std(var2_ready, rstd2_ready, mv2, var2, rstd2, B - 1)
            scatter(B - 1)
            hold(pool, sent, 64 * B + 16 * CLEARS)

        @block.scalar
        def _(act):
            def weights(n):
                act.wait_ge(w_in[n], 16)
                nc.scalar.copy(w_hl[w_order[n][0]][:, 0], w_tmp[n]).then_inc(w_hi, 1)

            for n in range(3):
                weights(n)

            def k_split(b, g, h):
                if h == 0:
                    if g == 0:
                        later(act, kst_in[1], KQ * 2 * b)
                    elif g == 1:
                        act.wait_ge(kst_in[0], KQ * (2 * b + 1))
                    elif g == 2:
                        act.wait_ge(qst_in, KQ * (b + 1))
                    else:
                        act.wait_ge(kst_in[1], KQ * (2 * b + 1))
                act.wait_ge(k_proj, 8 * b + 2 * g + h + 1)
                bank = k_bank(g, h)
                nc.scalar.copy(kq_hl[:, K_BUF[g], 0, h * HALF:(h + 1) * HALF], bank[:, h:h + HALF]).then_inc(k_hi, 1)

            def turned(b, i, source, done, sem_in):
                act.wait_ge(sem_in, 2 * b + i + 1)
                dst = tok_hl[:, 0, :, i * TP:(i + 1) * TP]
                nc.scalar.copy(dst, source[:, 0:KC * TP].rearrange("p (c t) -> p c t", t=TP)).then_inc(done, 1)

            def values(b, t):
                act.wait_ge(v_proj, NS * b + t + 1)
                nc.scalar.copy(v_sb[0:SP, t, :], v_bank(t)[0:SP, :]).then_inc(v_ready, 1)

            def queries(b, i):
                act.wait_ge(q_proj, 2 * b + i + 1)
                if i == 0 and not (isinstance(b, int) and b == 0):
                    act.wait_ge(kst_in[0], KQ * 2 * b)
                nc.scalar.activation(kq_hl[:, Q_BUF, 0, 2 * L * i:2 * L * (i + 1)], q_bank[i][:, 0:2 * L],
                                     ACT.Copy, scale=SCALE).then_inc(q_hi, 1)

            def sigmoid(b, i):
                act.wait_ge(scores_out, NI * b + i + 1)
                nc.scalar.activation(probs[0:SP, i % 3].rearrange("p (a h) l -> p a (h l)", a=2),
                                     ps_s[0:SP, i % 2, :, 0:2 * L], ACT.Sigmoid).then_inc(probs_ready, 1)

            def attended(b, g):
                act.wait_ge(pv_out, NI * b + NS * (g + 1))
                nc.scalar.copy(o_hl[:, 0, g, :], o_out(g)[:, 0:L]).then_inc(o_hi, 1)

            def router(r):
                act.wait_ge(z_ready, r + 1)
                nc.scalar.activation(sgp[:], zed[:], ACT.Sigmoid).then_inc(router_sig, 1)
                nc.scalar.activation(sgn[:], zed[:], ACT.Sigmoid, scale=-1.0).then_inc(router_sig, 1)

            def body(b, first=False, last=False):
                if first:
                    k_split(b, 0, 0)
                k_split(b, 0, 1)
                for t in (0, 1, 2):
                    values(b, t)
                if first:
                    for i in range(NT):
                        turned(0, i, turn_bank[i], xnt_hi, xn_turned)
                    for i in range(2):
                        queries(0, i)
                    weights(3)
                k_split(b, 1, 0)
                k_split(b, 1, 1)
                for t in (3, 4, 5):
                    values(b, t)
                if first:
                    act.wait_ge(w_lo, 4)
                for i in range(NI):
                    sigmoid(b, i)
                    if i in (2, 5, 8, 11):
                        k_split(b, 2 + i // 6, (i // 3) % 2)
                    if i in (7, 13, 19):
                        attended(b, i // 6 - 1)
                    if not first and i in (0, 1):
                        turned(b - 1, i, x2_bank[i], x2t_hi, x2_turned)
                    if not first and i == 9:
                        router(b - 1)
                    if not last and i == 11:
                        turned(b + 1, 0, turn_bank[0], xnt_hi, xn_turned)
                        turned(b + 1, 1, turn_bank[1], xnt_hi, xn_turned)
                    if not last and i in (15, 17):
                        queries(b + 1, i // 17)
                if not last:
                    k_split(b + 1, 0, 0)
                attended(b, G - 1)

            body(0, first=True)
            with act.Fori(1, B - 1) as b:
                body(b)
            body(B - 1, last=True)
            turned(B - 1, 0, ps_c, x2t_hi, x2_turned)
            turned(B - 1, 1, ps_b, x2t_hi, x2_turned)
            router(B - 1)

        @block.vector
        def _(dve):
            v = nc.vector
            link = Links(dve, dve_link)

            def less(dst, whole, hi, scale=None):
                if scale is None:
                    return v.tensor_tensor(dst, whole, hi.bitcast(F32), ALU.subtract)
                return v.scalar_tensor_tensor(out=dst, in0=whole, scalar=scale, in1=hi.bitcast(F32),
                                              op0=ALU.mult, op1=ALU.subtract)

            v.memset(cum[:], 0.0).then_inc(counts_read, 1)

            def split_lo(b, chunks=range(KC)):
                for k in chunks:
                    dve.wait_ge(ctx_hi, 4 * b + k + 1)
                    less(ctx_hl[:, 1, k, :], ctx_raw(k), ctx_hl[:, 0, k, :]).then_inc(ctx_lo, 1)

            def norm_stats(src, st, mv, ready, waits=()):
                for s, c in waits:
                    later(dve, s, c)
                for i in range(NT):
                    link(v.bn_stats(st[:, i, :], src(i)))
                hold(dve, dve_link, link.count())
                for i in range(NT):
                    ins = v.bn_aggr(mv[:, i, :], st[:, i, :])
                    if i < NT - 1:
                        link(ins)
                    else:
                        ins.then_inc(ready, 1)

            def norm1_stats(b):
                norm_stats(lambda i: x_in[:, i, :], st1, mv1, var1_ready, ((x_in_s, 16 * (b + 1)),))

            def norm1(b):
                dve.wait_ge(rstd1_ready, b + 1)
                for i in range(NT):
                    v.tensor_scalar(x_in[:, i, :], x_in[:, i, :], mv1[:, i, 0:1], rstd1[:, i:i + 1],
                                    ALU.subtract, ALU.mult).then_inc(xn_ready, 1)

            def k_split(b, g, h):
                dve.wait_ge(k_hi, 8 * b + 2 * g + h + 1)
                cols = slice(h * HALF, (h + 1) * HALF)
                less(kq_hl[:, K_BUF[g], 1, cols], k_bank(g, h)[:, h:h + HALF],
                     kq_hl[:, K_BUF[g], 0, cols]).then_inc(k_lo, 1)

            def turned(b, i, source, ready, done):
                dve.wait_ge(ready, 2 * b + i + 1)
                cols = slice(i * TP, (i + 1) * TP)
                less(tok_hl[:, 1, :, cols], source[:, 0:KC * TP].rearrange("p (c t) -> p c t", t=TP),
                     tok_hl[:, 0, :, cols]).then_inc(done, 1)

            def queries(b, i):
                dve.wait_ge(q_hi, 2 * b + i + 1)
                cols = slice(2 * L * i, 2 * L * (i + 1))
                less(kq_hl[:, Q_BUF, 1, cols], q_bank[i][:, 0:2 * L], kq_hl[:, Q_BUF, 0, cols], SCALE).then_inc(q_lo, 1)

            def attended(b, g):
                dve.wait_ge(o_hi, G * b + g + 1)
                less(o_hl[:, 1, g, :], o_out(g)[:, 0:L], o_hl[:, 0, g, :]).then_inc(o_lo, 1)

            def residual(r, i, banks=o_bank):
                if i == 0:
                    dve.wait_ge(sent, 64 * r + 16 * CLEARS)
                    dve.wait_ge(xres_in, 16 * (r + 1))
                dve.wait_ge(wo_out, 2 * r + i + 1)
                v.tensor_tensor(rows[:, i, D:2 * D], banks[i][0:TP, 0:D], x_res[:, i, :],
                                ALU.add).then_inc(x2_ready, 1)

            def norm2_stats(r):
                norm_stats(lambda i: rows[:, i, D:2 * D], st2, mv2, var2_ready, ((x2_ready, 2 * r + 2),))

            def norm2(r):
                dve.wait_ge(rstd2_ready, r + 1)
                for i in range(NT):
                    v.tensor_scalar(xn2[:, i, :], rows[:, i, D:2 * D], mv2[:, i, 0:1], rstd2[:, i:i + 1],
                                    ALU.subtract, ALU.mult).then_inc(xn2_ready, 1)

            def wide(t, n=E):
                return t[:, :, None].broadcast_to([TP, NT, n])

            mx, best, tot, rtot, pmax, rpmax, factor, pos, eslot, kept, place, spare = (red[:, n, :] for n in range(12))
            base = cst[0:TP, C_BASE:C_BASE + NT * E].rearrange("p (i e) -> p i e", e=E)
            rank = cst[0:TP, C_RANK:C_RANK + NT * E].rearrange("p (i e) -> p i e", e=E)
            token = cst[0:TP, C_TOK:C_TOK + NT]

            def choose(r, bank):
                dve.wait_ge(logits_out, r + 1)
                lo = bank[0:TP, 0:NT * P].rearrange("p (i n) -> p i n", n=P)
                link(v.tensor_tensor(lg0[:], lo[:, :, 0:E], bsw[:], ALU.add))
                link.done()
                link(v.tensor_tensor(lg[:], lo[:, :, E:2 * E], lg0[:], ALU.add))
                link.done()
                link(v.tensor_reduce(mx, lg[:], AX_X, ALU.max))
                link.done()
                v.tensor_tensor(zed[:], lg[:], wide(mx), ALU.subtract).then_inc(z_ready, 1)
                link(v.tensor_tensor(cand[:], lg[:], wide(mx), ALU.is_equal))
                link.done()
                link(v.tensor_tensor(cand[:], cand[:], rank, ALU.mult))
                link.done()
                link(v.tensor_reduce(best, cand[:], AX_X, ALU.max))
                link.done()
                v.tensor_tensor(hot16[:], cand[:], wide(best), ALU.is_equal).then_inc(hot_ready, 1)
                link(v.tensor_tensor(hot[:], cand[:], wide(best), ALU.is_equal))

            def scale_tokens(r):
                dve.wait_ge(router_sig, 2 * r + 2)
                link(v.reciprocal(sgn[:], sgn[:]))
                link.done()
                link(v.tensor_tensor(prb[:], sgp[:], sgn[:], ALU.mult))
                link.done()
                link(v.tensor_reduce(tot, prb[:], AX_X, ALU.add))
                link.done()
                link(v.reciprocal(rtot, tot))
                link.done()
                link(v.tensor_tensor(prb[:], prb[:], wide(rtot), ALU.mult))
                link.done()
                link(v.tensor_reduce(pmax, prb[:], AX_X, ALU.max))
                link.done()
                link(v.reciprocal(rpmax, pmax))
                link.done()
                link(v.tensor_tensor(factor, pmax, rpmax, ALU.mult))
                link.done()
                for i in range(NT):
                    link(v.tensor_scalar(rows[:, i, 0:D], xn2[:, i, :], factor[:, i:i + 1], None, ALU.mult))

            def place_tokens(r, bank):
                dve.wait_ge(pos_out, r + 1)
                link.done()
                bank = bank[:, 2 * L:512]
                before = bank[0:TP, 0:NT * E].rearrange("p (i e) -> p i e", e=E)
                dve.wait_ge(counts_read, r + 1)
                link(v.tensor_tensor(posb[:], before, cum[:, None, :].broadcast_to([TP, NT, E]), ALU.add))
                link(v.tensor_tensor(eoff[:], hot[:], base, ALU.mult))
                link.done()
                v.tensor_tensor(cum[:], bank[0:TP, NT * E:(NT + 1) * E], cum[:], ALU.add).then_inc(counts_read, 1)
                link(v.tensor_tensor(posb[:], posb[:], hot[:], ALU.mult))
                link(v.tensor_reduce(eslot, eoff[:], AX_X, ALU.add))
                link.done()
                link(v.tensor_reduce(pos, posb[:], AX_X, ALU.add))
                link.done()
                link(v.tensor_scalar(spare, pos, float(CAP), NOWHERE, ALU.is_ge, ALU.mult))
                link(v.tensor_scalar(kept, pos, float(CAP), NOWHERE, ALU.is_lt, ALU.mult))
                link(v.tensor_tensor(place, pos, eslot, ALU.add))
                link.done()
                link(v.tensor_tensor(slot_i[:], place, spare, ALU.add))
                link(v.tensor_tensor(drop_i[:], token, kept, ALU.add))
                link(v.tensor_copy(rows[:, :, 2 * D].bitcast(I32), token))
                link(v.tensor_scalar(token, token, float(L), None, ALU.add))
                link(v.tensor_tensor(xn2[:, 0, :], rows[:, 0, 0:D], rows[:, 0, D:2 * D], ALU.add))
                link.done()
                v.tensor_tensor(xn2[:, 1, :], rows[:, 1, 0:D], rows[:, 1, D:2 * D], ALU.add).then_inc(rows_ready, 1)

            dve.wait_ge(w_hi, 1)
            less(w_hl["k"][:, 1], w_tmp[0], w_hl["k"][:, 0]).then_inc(w_lo, 1)
            for k in range(KC):
                if k < 2:
                    dve.wait_ge(raw_in[k], 16)
                    v.tensor_copy(ctx_hl[:, 0, k, :], ctx_raw(k)).then_inc(first_hi, 1)
                    dve.wait_ge(first_hi, k + 1)
                else:
                    dve.wait_ge(ctx_hi, 2 * (k - 1))
                less(ctx_hl[:, 1, k, :], ctx_raw(k), ctx_hl[:, 0, k, :]).then_inc(ctx_lo, 1)
            for n in (1, 2):
                name = w_order[n][0]
                dve.wait_ge(w_hi, n + 1)
                less(w_hl[name][:, 1], w_tmp[n], w_hl[name][:, 0]).then_inc(w_lo, 1)
            dve.wait_ge(w_lo, 3)
            v.memset(rows[:, 0, 0:2 * D], 0.0).then_inc(cleared, 1)
            v.memset(rows[:, 0, 2 * D:ROW].bitcast(I32), int(NOWHERE)).then_inc(cleared, 1)
            v.memset(rows[:, 1, 2 * D:ROW].bitcast(I32), 0).then_inc(prep, 1)
            def last_tables():
                dve.wait_ge(w_hi, 4)
                less(w_hl["o"][:, 1], w_tmp[3], w_hl["o"][:, 0]).then_inc(w_lo, 1)
                dve.wait_ge(cst_in, 16)
                dve.wait_ge(router_in, 32)
                v.memset(sw_hl[:].bitcast(I32), 0).then_inc(prep, 1)
                dve.wait_ge(prep, 2)
                v.tensor_copy(sw_hl[:, :, 0:E], sw_raw[:]).then_inc(prep, 1)
                dve.wait_ge(prep, 3)
                less(sw_hl[:, :, E:2 * E], sw_raw[:], sw_hl[:, :, 0:E]).then_inc(prep, 1)
                v.tensor_copy(low16[:], cst[0:TP, C_LOW:C_LOW + TP]).then_inc(prep, 1)
                v.tensor_copy(one16[:], cst[0:TP, C_ONE:C_ONE + TP]).then_inc(prep, 1)

            def body(b, first=False, last=False):
                if first:
                    k_split(b, 0, 0)
                k_split(b, 0, 1)
                if not first:
                    residual(b - 1, 0)
                    residual(b - 1, 1)
                    norm2_stats(b - 1)
                    norm2(b - 1)
                else:
                    norm1_stats(0)
                    norm1(0)
                    for i in range(NT):
                        turned(0, i, turn_bank[i], xnt_hi, xnt_lo)
                    for i in range(2):
                        queries(0, i)
                if first:
                    last_tables()
                k_split(b, 1, 0)
                k_split(b, 1, 1)
                if not last:
                    norm1_stats(b + 1)
                    norm1(b + 1)
                if not first:
                    turned(b - 1, 0, x2_bank[0], x2t_hi, x2t_lo)
                k_split(b, 2, 0)
                if not first:
                    turned(b - 1, 1, x2_bank[1], x2t_hi, x2t_lo)
                k_split(b, 2, 1)
                attended(b, 0)
                if not first:
                    choose(b - 1, ps_b)
                k_split(b, 3, 0)
                k_split(b, 3, 1)
                if not last:
                    turned(b + 1, 0, turn_bank[0], xnt_hi, xnt_lo)
                    turned(b + 1, 1, turn_bank[1], xnt_hi, xnt_lo)
                attended(b, 1)
                if not first:
                    scale_tokens(b - 1)
                if not last:
                    split_lo(b + 1, (0, 1))
                    queries(b + 1, 0)
                    split_lo(b + 1, (2, 3))
                    queries(b + 1, 1)
                attended(b, 2)
                if not first:
                    place_tokens(b - 1, ps_b)
                if not last:
                    k_split(b + 1, 0, 0)
                attended(b, 3)

            body(0, first=True)
            start = link.n
            with dve.Fori(1, B - 1) as b:
                link.base, link.n = start + MID_LINKS * (b - 1), 0
                body(b)
                assert link.n == MID_LINKS, link.n
            link.base, link.n = start + MID_LINKS * (B - 2), 0
            body(B - 1, last=True)
            residual(B - 1, 0, (ps_b, ps_a))
            residual(B - 1, 1, (ps_b, ps_a))
            norm2_stats(B - 1)
            norm2(B - 1)
            turned(B - 1, 0, ps_c, x2t_hi, x2t_lo)
            turned(B - 1, 1, ps_b, x2t_hi, x2t_lo)
            choose(B - 1, ps_a)
            scale_tokens(B - 1)
            place_tokens(B - 1, ps_c)
            dve.wait_ge(counts_read, B + 1)
            v.tensor_copy(loads[:], cum[0:1, :]).then_inc(loads_ready, 1)
            dve.wait_ge(loads_ready, 1)

        @block.tensor
        def _(pe):
            mm = nc.tensor.matmul

            def project_k(b, g, h, part=None):
                bank = k_bank(g, h)
                chunks = range(KC) if part is None else ((0,), (1,), (2, 3))[part]
                for k in chunks:
                    if g == 0 and h == 0:
                        pe.wait_ge(ctx_lo, 4 * b + k + 1)
                    for n, (a, c) in enumerate(three):
                        last = mm(bank[:, 0:HALF + 1], w_hl["k"][:, a, k, g * P:(g + 1) * P],
                                  ctx_hl[:, c, k, h * (HALF - 1):h * (HALF - 1) + HALF + 1],
                                  start=(k == 0 and n == 0), stop=(k == KC - 1 and n == 2))
                if part in (None, 2):
                    last.then_inc(k_proj, 1)

            def project_v(b, t):
                for k in range(KC):
                    for n, (a, c) in enumerate(three):
                        last = mm(v_bank(t)[0:SP, :], ctx_hl[:, a, k, t * SP:(t + 1) * SP], w_hl["v"][:, c, k, :],
                                  start=(k == 0 and n == 0), stop=(k == KC - 1 and n == 2))
                last.then_inc(v_proj, 1)

            def project_q(b, i, parts=(0, 1)):
                for part in parts:
                    g = 2 * i + part
                    for k in range(KC):
                        for n, (a, c) in enumerate(three):
                            last = mm(q_bank[i][:, part * L:(part + 1) * L], w_hl["q"][:, a, k, g * P:(g + 1) * P],
                                      tok_hl[:, c, k, :], start=(k == 0 and n == 0), stop=(k == KC - 1 and n == 2))
                if 1 in parts:
                    last.then_inc(q_proj, 1)

            def project_o(r, i, bank):
                for g in range(G):
                    for n, (a, c) in enumerate(three):
                        last = mm(bank[0:TP, :], o_hl[:, a, g, i * TP:(i + 1) * TP], w_hl["o"][:, c, g, :],
                                  start=(g == 0 and n == 0), stop=(g == G - 1 and n == 2))
                last.then_inc(wo_out, 1)

            def turn(src, i, bank, done):
                for k in range(KC):
                    last = nc.tensor.transpose(bank[:, k * TP:(k + 1) * TP], src[:, i, k * P:(k + 1) * P], ident)
                last.then_inc(done, 1)

            def scores(b, i):
                g, t = divmod(i, NS)
                if t == 0:
                    pe.wait_ge(kst_in[g % 2], KQ * (2 * b + g // 2 + 1))
                if i == 0:
                    pe.wait_ge(qst_in, KQ * (b + 1))
                later(pe, probs_ready, NI * b + i - 1)
                for j in range(4):
                    last = mm(ps_s[0:SP, i % 2, j // 2, (j % 2) * L:(j % 2 + 1) * L],
                              k_st[0:96, g % 2, j, t * SP:(t + 1) * SP], q_st[0:96, j, g, :],
                              start=True, stop=True)
                last.then_inc(scores_out, 1)

            def attend(b, i, last=False):
                g, t = divmod(i, NS)
                if i == 0:
                    pe.wait_ge(v_ready, NS * (b + 1))
                if t == 0:
                    if g < G - 1:
                        later(pe, o_lo, G * b + g)
                    elif last:
                        pe.wait_ge(k_lo, 8 * b + 7)
                pe.wait_ge(probs_ready, NI * b + i + 1)
                for j in range(4):
                    h = 4 * g + j
                    done = mm(o_out(g)[HD * j:HD * (j + 1), 0:L], v_sb[0:SP, t, HD * h:HD * (h + 1)],
                              probs[0:SP, i % 3, j, :], start=(t == 0), stop=(t == NS - 1))
                done.then_inc(pv_out, 1)

            def route(r, bank):
                pe.wait_ge(x2t_lo, 2 * r + 2)
                for i in range(NT):
                    for k in range(KC):
                        for a in (0, 1):
                            last = mm(bank[0:TP, i * P:(i + 1) * P], tok_hl[:, a, k, i * TP:(i + 1) * TP],
                                      sw_hl[:, k, :], start=(k == 0 and a == 0), stop=(k == KC - 1 and a == 1))
                last.then_inc(logits_out, 1)

            def count(r, bank):
                pe.wait_ge(hot_ready, r + 1)
                bank = bank[:, 2 * L:512]
                mm(bank[0:TP, 0:E], low16[:], hot16[:, 0, :], start=True, stop=True)
                mm(bank[0:TP, E:2 * E], low16[:], hot16[:, 1, :], start=True, stop=False)
                mm(bank[0:TP, E:2 * E], one16[:], hot16[:, 0, :], start=False, stop=True)
                mm(bank[0:TP, 2 * E:3 * E], one16[:], hot16[:, 0, :], start=True, stop=False)
                mm(bank[0:TP, 2 * E:3 * E], one16[:], hot16[:, 1, :], start=False, stop=True).then_inc(pos_out, 1)

            def body(b, first=False, last=False):
                if first:
                    pe.wait_ge(w_lo, 1)
                    project_k(b, 0, 0)
                else:
                    pe.wait_ge(q_lo, 2 * b + 2)
                    pe.wait_ge(counts_read, b)
                project_k(b, 0, 1)
                if not first:
                    pe.wait_ge(o_lo, G * b)
                    project_o(b - 1, 0, o_bank[0])
                    pe.wait_ge(k_lo, 8 * b + 1)
                    project_o(b - 1, 1, o_bank[1])
                else:
                    pe.wait_ge(w_lo, 2)
                pe.wait_ge(k_lo, 8 * b + 2)
                project_v(b, 0)
                if not first:
                    pe.wait_ge(x2_ready, 2 * b - 1)
                project_v(b, 1)
                if not first:
                    pe.wait_ge(x2_ready, 2 * b)
                project_v(b, 2)
                if first:
                    pe.wait_ge(cst_in, 16)
                    for i in range(NT):
                        pe.wait_ge(xn_ready, i + 1)
                        pe.wait_ge(v_ready, 1 + i)
                        turn(x_in, i, turn_bank[i], xn_turned)
                    pe.wait_ge(w_lo, 3)
                    pe.wait_ge(v_ready, 3)
                    pe.wait_ge(xnt_lo, 2)
                    project_q(0, 0)
                    project_q(0, 1)
                    pe.wait_ge(q_lo, 2)
                pe.wait_ge(v_ready, NS * b + 1)
                project_k(b, 1, 0)
                pe.wait_ge(v_ready, NS * b + 2)
                project_k(b, 1, 1)
                pe.wait_ge(v_ready, NS * b + 3)
                project_v(b, 3)
                pe.wait_ge(k_lo, 8 * b + 3)
                project_v(b, 4)
                pe.wait_ge(k_lo, 8 * b + 4)
                project_v(b, 5)
                for i in range(NI):
                    scores(b, i)
                    if not first:
                        if i == 0:
                            pe.wait_ge(v_ready, NS * b + 4)
                            pe.wait_ge(xn2_ready, 2 * b - 1)
                            turn(xn2, 0, x2_bank[0], x2_turned)
                            pe.wait_ge(v_ready, NS * b + 5)
                        if i == 1:
                            pe.wait_ge(v_ready, NS * b + 6)
                            pe.wait_ge(xn2_ready, 2 * b)
                            turn(xn2, 1, x2_bank[1], x2_turned)
                        if i == 3:
                            pe.wait_ge(x2t_lo, 2 * b - 1)
                        if i == 6:
                            pe.wait_ge(k_lo, 8 * b + 5)
                            route(b - 1, ps_b)
                    elif i == 0:
                        pe.wait_ge(v_ready, 5)
                    elif i == 6:
                        pe.wait_ge(v_ready, 6)
                    if i == 9:
                        pe.wait_ge(k_lo, 8 * b + 6)
                    if i < 12:
                        project_k(b, 2 + i // 6, (i // 3) % 2, i % 3)
                    if not last:
                        if i == 11:
                            if first:
                                pe.wait_ge(k_lo, 5)
                            else:
                                pe.wait_ge(hot_ready, b)
                            pe.wait_ge(xn_ready, 2 * b + 3)
                            turn(x_in, 0, turn_bank[0], xn_turned)
                        if i == 11:
                            pe.wait_ge(k_lo, 8 * b + 7)
                            pe.wait_ge(xn_ready, 2 * b + 4)
                            turn(x_in, 1, turn_bank[1], xn_turned)
                        if i == 14:
                            pe.wait_ge(k_lo, 8 * b + 8)
                            pe.wait_ge(xnt_lo, 2 * b + 4)
                    if not first and i == 17:
                        count(b - 1, ps_b)
                    if not last:
                        if 14 <= i < 18:
                            project_q(b + 1, (i - 14) // 2, (i % 2,))
                    if i >= 2:
                        attend(b, i - 2, last)
                if not last:
                    pe.wait_ge(q_lo, 2 * b + 3)
                    project_k(b + 1, 0, 0)
                attend(b, NI - 2)
                attend(b, NI - 1)

            body(0, first=True)
            pe.wait_ge(w_lo, 4)
            pe.wait_ge(prep, 6)
            with pe.Fori(1, B - 1) as b:
                body(b)
            body(B - 1, last=True)
            r = B - 1
            pe.wait_ge(k_lo, 8 * B)
            pe.wait_ge(o_lo, G * B)
            project_o(r, 0, ps_b)
            project_o(r, 1, ps_a)
            pe.wait_ge(xn2_ready, 2 * r + 1)
            turn(xn2, 0, ps_c, x2_turned)
            pe.wait_ge(xn2_ready, 2 * r + 2)
            turn(xn2, 1, ps_b, x2_turned)
            route(r, ps_a)
            count(r, ps_c)


def expert_phase(nc, sh, w1, w2, b1, b2, consts, slots, loads, out):
    D, KC, TP, ROW, E, CAP, T, CH, FC = sh.D, sh.KC, sh.TP, sh.ROW, sh.E, sh.CAP, sh.T, sh.CH, sh.FC
    NST = CAP // TP
    NF = FC // P
    FT = CH * NF

    with ExitStack() as ctx:
        def sb(name, shape, dt=F32):
            return ctx.enter_context(nc.sbuf_tensor(name, shape, dt))

        def sem(name):
            return ctx.enter_context(nc.semaphore(name))

        ps_y = ctx.enter_context(nc.psum_tensor("ps_y", [P, 4, 512], F32))
        ps_h = ctx.enter_context(nc.psum_tensor("ps_h", [P, 4, 512], F32))

        idt = sb("idt", [TP, TP])
        b1_sb = sb("b1_sb", [P, E, FT])
        b1s = sb("b1s", [P, E, FT])
        b2_sb = sb("b2_sb", [TP, 2, D])
        xs_in = sb("xs_in", [TP, NST, D])
        res = sb("res", [TP, NST, D + 4])
        res_b = sb("res_b", [TP, NST, D])
        tok = sb("tok", [TP, NST], I32)
        xs_hl = sb("xs_hl", [P, 2, KC, CAP], F32R)
        w1_raw = sb("w1_raw", [P, 4, KC, FC])
        w2_raw = sb("w2_raw", [P, 4, NF, D])
        w1_hl = sb("w1_hl", [P, 2, 2, KC, FC], F32R)
        w2_hl = sb("w2_hl", [P, 2, 2, NF, D], F32R)
        hid = sb("hid", [P, 2, CAP])
        hid_hl = sb("hid_hl", [P, 4, 2, CAP], F32R)
        y_sb = sb("y_sb", [TP, NST, D])

        cst_in = sem("cst_in2")
        xs_in_s, res_in, b2_in = sem("xs_in_s"), sem("res_in"), sem("b2_in")
        w1_in = [sem(f"w1_in{i}") for i in range(4)]
        w2_in = [sem(f"w2_in{i}") for i in range(4)]
        stored = sem("stored")
        b1_scaled = sem("b1_scaled")
        xs_turned, xs_hi, xs_lo = sem("xs_turned"), sem("xs_hi"), sem("xs_lo")
        w1_hi, w1_lo, w2_hi, w2_lo = sem("w1_hi"), sem("w1_lo"), sem("w2_hi"), sem("w2_lo")
        h_out, gelu_done, h_hi, h_lo = sem("h_out"), sem("gelu_done"), sem("h_hi"), sem("h_lo")
        y_chunk, y_ready, y_cleared = sem("y_chunk"), sem("y_ready"), sem("y_cleared")
        res_ready = sem("res_ready")

        three = ((0, 0), (0, 1), (1, 0))

        def hold(eng, s, count):
            wait_alone(eng, s, count, b1_scaled)

        def after(eng, s, count):
            if not (isinstance(count, int) and count <= 0):
                hold(eng, s, count)

        block = ctx.enter_context(nc.Block())

        def slot_rows(e):
            return slots.rearrange("(e i p) c -> e p i c", e=E, p=TP)[e]

        @block.sync
        def _(sp):
            def load_chunk(e, c):
                if not (isinstance(e, int) and e == 0 and c < 4):
                    hold(sp, w1_lo, CH * e + c - 3)
                    hold(sp, w2_lo, CH * e + c - 3)
                sp.dma_start(w1_raw[:, c % 4], w1[e, c]).then_inc(w1_in[c % 4], 16)
                sp.dma_start(w2_raw[:, c % 4], w2[e, c]).then_inc(w2_in[c % 4], 16)

            def load_slots(e):
                after(sp, xs_turned, KC * e)
                sp.dma_start(xs_in[:], slot_rows(e)[:, :, 0:D]).then_inc(xs_in_s, 16)

            def load_residual(e):
                after(sp, res_ready, 2 * e)
                sp.dma_start(res[:], slot_rows(e)[:, :, D:ROW]).then_inc(res_in, 16)
                sp.dma_start(b2_sb[:, 0, :], b2[e].partition_broadcast(TP)).then_inc(b2_in, 16)

            load_slots(0)
            sp.dma_start(idt[:], consts[0:TP, C_ID:C_ID + TP]).then_inc(cst_in, 16)
            sp.dma_start(b1_sb[:], b1).then_inc(cst_in, 16)
            for c in range(4):
                load_chunk(0, c)
            load_residual(0)

            def body(e, last=False):
                for c in range(4, CH):
                    load_chunk(e, c)
                    if c == 5 and not last:
                        load_slots(e + 1)
                if not last:
                    for c in range(4):
                        load_chunk(e + 1, c)
                    load_residual(e + 1)

            with sp.Fori(0, E - 1) as e:
                body(e)
            body(E - 1, last=True)

        @block.gpsimd
        def _(pool):
            def store(e):
                for i in range(NST):
                    hold(pool, y_ready, NST * e + i + 1)
                    pool.indirect_dma_start(
                        out=out, out_offset=bass.IndirectOffsetOnAxis(ap=tok[:, i:i + 1].bitcast(U32), axis=0),
                        in_=y_sb[:, i, :], in_offset=None, bounds_check=T - 1, oob_is_err=False).then_inc(stored, 16)

            def body(e, first=False):
                if not first:
                    store(e - 1)
                hold(pool, res_in, 16 * (e + 1))
                hold(pool, b2_in, 16 * (e + 1))
                if not first:
                    hold(pool, stored, 16 * NST * e)
                nc.gpsimd.tensor_copy(tok[:], res[:, :, D].bitcast(I32)).then_inc(res_ready, 1)
                nc.gpsimd.tensor_tensor(res_b[:], res[:, :, 0:D], b2_sb[:, 0:1, :].broadcast_to([TP, NST, D]),
                                        ALU.add).then_inc(res_ready, 1)

            body(0, first=True)
            with pool.Fori(1, E) as e:
                body(e)
            store(E - 1)
            hold(pool, stored, 16 * NST * E)

        @block.scalar
        def _(act):
            act.wait_ge(cst_in, 32)
            nc.scalar.activation(b1s[:], b1_sb[:], ACT.Copy, scale=STRETCH).then_inc(b1_scaled, 1)
            act.wait_ge(b1_scaled, 1)

            def split_w1(e, c):
                act.wait_ge(w1_in[c % 4], 16 * (2 * e + c // 4 + 1))
                if not (isinstance(e, int) and e == 0 and c < 2):
                    act.wait_ge(h_out, FT * e + NF * (c - 1))
                nc.scalar.copy(w1_hl[:, c % 2, 0], w1_raw[:, c % 4]).then_inc(w1_hi, 1)

            def split_w2(e, c):
                act.wait_ge(w2_in[c % 4], 16 * (2 * e + c // 4 + 1))
                if not (isinstance(e, int) and e == 0 and c < 2):
                    act.wait_ge(y_chunk, CH * e + c - 1)
                nc.scalar.copy(w2_hl[:, c % 2, 0], w2_raw[:, c % 4]).then_inc(w2_hi, 1)

            def split_slots(e):
                for k in range(KC):
                    act.wait_ge(xs_turned, KC * e + k + 1)
                    nc.scalar.copy(xs_hl[:, 0, k, :], ps_h[:, k, 0:CAP]).then_inc(xs_hi, 1)

            def gelu(e, f):
                act.wait_ge(h_out, FT * e + f + 1)
                if not (isinstance(e, int) and e == 0 and f < 2):
                    act.wait_ge(h_lo, FT * e + f - 1)
                nc.scalar.activation(hid[:, f % 2, :], ps_h[:, f % 4, 0:CAP], ACT.Gelu,
                                     bias=b1s[:, e, f:f + 1],
                                     scale=STRETCH).then_inc(gelu_done, 1)

            def body(e, last=False):
                for c in range(CH):
                    if not (last and c == CH - 1):
                        split_w1(e + (c + 1) // CH, (c + 1) % CH)
                    for f in (NF * c, NF * c + 1):
                        gelu(e, f)
                    if c == CH - 1 and not last:
                        split_slots(e + 1)
                    if not (last and c == CH - 1):
                        split_w2(e + (c + 1) // CH, (c + 1) % CH)

            split_w1(0, 0)
            split_slots(0)
            split_w2(0, 0)
            body(0)
            with act.Fori(1, E - 1) as e:
                body(e)
            body(E - 1, last=True)

        @block.vector
        def _(dve):
            v = nc.vector

            def less(dst, whole, hi):
                return v.tensor_tensor(dst, whole, hi.bitcast(F32), ALU.subtract)

            def split_w1(e, c):
                dve.wait_ge(w1_hi, CH * e + c + 1)
                less(w1_hl[:, c % 2, 1], w1_raw[:, c % 4], w1_hl[:, c % 2, 0]).then_inc(w1_lo, 1)

            def split_w2(e, c):
                dve.wait_ge(w2_hi, CH * e + c + 1)
                less(w2_hl[:, c % 2, 1], w2_raw[:, c % 4], w2_hl[:, c % 2, 0]).then_inc(w2_lo, 1)

            def split_slots(e):
                for k in range(KC):
                    dve.wait_ge(xs_hi, KC * e + k + 1)
                    less(xs_hl[:, 1, k, :], ps_h[:, k, 0:CAP], xs_hl[:, 0, k, :]).then_inc(xs_lo, 1)

            def split_hidden(e, f):
                dve.wait_ge(gelu_done, FT * e + f + 1)
                if not (isinstance(e, int) and e == 0 and f < 4):
                    dve.wait_ge(y_chunk, CH * e + f // 2 - 1)
                v.tensor_copy(hid_hl[:, f % 4, 0, :], hid[:, f % 2, :]).then_inc(h_hi, 1)
                dve.wait_ge(h_hi, FT * e + f + 1)
                less(hid_hl[:, f % 4, 1, :], hid[:, f % 2, :], hid_hl[:, f % 4, 0, :]).then_inc(h_lo, 1)

            def results(e):
                dve.wait_ge(y_chunk, CH * (e + 1))
                dve.wait_ge(res_ready, 2 * e + 2)
                for i in range(NST):
                    v.scalar_tensor_tensor(out=y_sb[:, i, :], in0=ps_y[0:TP, i, :], scalar=1.0 / STRETCH,
                                           in1=res_b[:, i, :], op0=ALU.mult, op1=ALU.add).then_inc(y_ready, 1)

            def body(e, first=False, last=False):
                for c in range(CH):
                    if not (last and c == CH - 1):
                        split_w1(e + (c + 1) // CH, (c + 1) % CH)
                    for f in (NF * c, NF * c + 1):
                        split_hidden(e, f)
                    if c == 0 and not first:
                        results(e - 1)
                    if c == CH - 1 and not last:
                        split_slots(e + 1)
                    if not (last and c == CH - 1):
                        split_w2(e + (c + 1) // CH, (c + 1) % CH)

            v.memset(ps_y[0:TP], 0.0).then_inc(y_cleared, 1)
            split_w1(0, 0)
            split_slots(0)
            split_w2(0, 0)
            body(0, first=True)
            with dve.Fori(1, E - 1) as e:
                body(e)
            body(E - 1, last=True)
            results(E - 1)

        @block.tensor
        def _(pe):
            mm = nc.tensor.matmul

            def turn_slots(e):
                pe.wait_ge(xs_in_s, 16 * (e + 1))
                for k in range(KC):
                    if not (isinstance(e, int) and e == 0):
                        pe.wait_ge(gelu_done, FT * e - KC + k + 1)
                    for i in range(NST):
                        last = nc.tensor.transpose(ps_h[:, k, i * TP:(i + 1) * TP], xs_in[:, i, k * P:(k + 1) * P], idt[:])
                    last.then_inc(xs_turned, 1)

            def hidden(e, c, tiles=NST):
                n_slots = tiles * TP
                pe.wait_ge(w1_lo, CH * e + c + 1)
                for m in range(NF):
                    f = NF * c + m
                    if c < 2:
                        pe.wait_ge(xs_lo, KC * (e + 1))
                    else:
                        pe.wait_ge(gelu_done, FT * e + f - 3)
                    for k in range(KC):
                        for n, (a, d) in enumerate(three):
                            last = mm(ps_h[:, f % 4, 0:n_slots], w1_hl[:, c % 2, a, k, m * P:(m + 1) * P],
                                      xs_hl[:, d, k, 0:n_slots], start=(k == 0 and n == 0), stop=(k == KC - 1 and n == 2))
                    last.then_inc(h_out, 1)

            def outputs(e, c, tiles, parts=range(NF)):
                if 0 in parts:
                    pe.wait_ge(w2_lo, CH * e + c + 1)
                for m in parts:
                    f = NF * c + m
                    pe.wait_ge(h_lo, FT * e + f + 1)
                    for i in range(tiles):
                        if f == 0 and not (isinstance(e, int) and e == 0):
                            pe.wait_ge(y_ready, NST * (e - 1) + i + 1)
                        for n, (a, d) in enumerate(three):
                            last = mm(ps_y[0:TP, i, :], hid_hl[:, f % 4, a, i * TP:(i + 1) * TP],
                                      w2_hl[:, c % 2, d, m, :], start=(f == 0 and n == 0), stop=(f == FT - 1 and n == 2))
                if NF - 1 in parts:
                    last.then_inc(y_chunk, 1)

            def arm(e, tiles, last):
                for c in range(CH - 2):
                    hidden(e, c + 1, tiles)
                    outputs(e, c, tiles)
                hidden(e, CH - 1, tiles)
                outputs(e, CH - 2, tiles, (0,))
                if not last:
                    turn_slots(e + 1)
                outputs(e, CH - 2, tiles, (1,))
                if not last:
                    hidden(e + 1, 0)
                outputs(e, CH - 1, tiles)

            def body(e, last=False):
                load = pe.value_load(loads[0:1, bass.ds(e, 1)])
                with pe.If(load <= TP):
                    arm(e, 1, last)
                with pe.Else():
                    with pe.If(load <= 3 * TP):
                        arm(e, 3, last)
                    with pe.Else():
                        arm(e, NST, last)

            pe.wait_ge(cst_in, 32)
            turn_slots(0)
            hidden(0, 0)
            pe.wait_ge(y_cleared, 1)
            body(0)
            with pe.Fori(1, E - 1) as e:
                body(e)
            body(E - 1, last=True)


def cross_attention_experts(nc, x, ctx_t, wq_t, wk_t, wv_t, wo_t, w_sw, b_sw, w1, b1, w2, b2, consts, out):
    sh = Shapes(x, ctx_t, w1, w2)
    slots = nc.dram_tensor("slots", (sh.T, sh.ROW), F32, kind="Internal").ap()
    out_rows = out.rearrange("b l d -> (b l) d")
    with nc.sbuf_tensor("loads", [1, sh.E], I32) as loads:
        attention_phase(nc, sh, x, ctx_t, wk_t, wv_t, wq_t, wo_t, w_sw, b_sw, consts, slots, loads, out_rows)
        expert_phase(nc, sh, w1, w2, b1, b2, consts, slots, loads, out_rows)


def _constants(tokens_per_tile, experts, capacity):
    import numpy as np

    tp = tokens_per_tile
    c = np.zeros((P, C_END), np.float32)
    c[:, C_ID:C_ID + P] = np.eye(P)
    c[:tp, C_LOW:C_LOW + tp] = np.triu(np.ones((tp, tp)), 1)
    c[:tp, C_ONE:C_ONE + tp] = 1
    c[:, C_BASE:C_BASE + 2 * experts] = np.tile(np.arange(experts) * capacity, 2)
    c[:, C_RANK:C_RANK + 2 * experts] = np.tile(experts - np.arange(experts), 2)
    c[:, C_TOK] = np.arange(P)
    c[:, C_TOK + 1] = np.arange(P) + tp
    return c


def kernel(x, ctx_1024, L0_xattn_Wq, L0_xattn_Wk, L0_xattn_Wv, L0_xattn_Wo, L0_ffn_W_sw, L0_ffn_b_sw,
           L0_ffn_W1, L0_ffn_b1, L0_ffn_W2, L0_ffn_b2):
    import numpy as np
    import concourse.bacc as bacc
    from concourse.bass_utils import run_bass_kernel_spmd

    B, L, D = x.shape
    S = ctx_1024.shape[1]
    E, _, F = L0_ffn_W1.shape
    KC, CH = D // P, F // 256

    def columns(w):
        return np.asarray(w).T.reshape(KC, P, -1).transpose(1, 0, 2)

    arrays = {
        "x": np.asarray(x),
        "ctx_t": np.asarray(ctx_1024).transpose(0, 2, 1).reshape(B, KC, P, S),
        "wq_t": columns(L0_xattn_Wq), "wk_t": columns(L0_xattn_Wk),
        "wv_t": columns(L0_xattn_Wv), "wo_t": columns(L0_xattn_Wo),
        "w_sw": np.asarray(L0_ffn_W_sw).reshape(KC, P, E).transpose(1, 0, 2),
        "b_sw": np.asarray(L0_ffn_b_sw),
        "w1": np.asarray(L0_ffn_W1).reshape(E, KC, P, CH, F // CH).transpose(0, 3, 2, 1, 4),
        "b1": np.asarray(L0_ffn_b1).reshape(E, F // P, P).transpose(2, 0, 1),
        "w2": np.asarray(L0_ffn_W2).reshape(E, CH, F // CH // P, P, D).transpose(0, 1, 3, 2, 4),
        "b2": np.asarray(L0_ffn_b2),
        "consts": _constants(112, E, B * L // E),
    }
    arrays = {n: np.ascontiguousarray(a) for n, a in arrays.items()}
    nc = bacc.Bacc("TRN2", target_bir_lowering=False, num_devices=1)
    ins = {n: nc.dram_tensor(n, a.shape, mybir.dt.from_np(a.dtype), kind="ExternalInput").ap() for n, a in arrays.items()}
    out = nc.dram_tensor("out", (B, L, D), F32, kind="ExternalOutput").ap()
    cross_attention_experts(nc, out=out, **ins)
    r = run_bass_kernel_spmd(nc, [arrays], core_ids=[0])
    return r.results[0]["out"]
```
